# Optimizing a Trainium2 kernel written in Bass

```python
import numpy as np
import jax
import jax.numpy as jnp

def _softmax(x, axis=-1):
    return jax.nn.softmax(x, axis=axis)

def _gelu(x):
    return jax.nn.gelu(x, approximate=True)

def _silu(x):
    return jax.nn.silu(x)

def _sigmoid(x):
    return jax.nn.sigmoid(x)

def _layernorm(x, axis=-1, eps=1e-05):
    m = jnp.mean(x, axis=axis, keepdims=True)
    v = jnp.var(x, axis=axis, keepdims=True)
    return (x - m) / jnp.sqrt(v + eps)

def _scatter_add(tgt, idx, src, axis=0):
    return tgt.at[idx].add(src)

def _segment_sum(src, seg, n):
    return jax.ops.segment_sum(src, seg, n)
kernel_name = 'mk_gnn_ffn_d1_gnn_r8_624727'

def setup_inputs(seed: int=0):
    np.random.seed(seed)
    _w = jnp.asarray

    def _rec_inputs():
        import jax
        import jax.numpy as jnp
        _gk = jax.random.key(seed)
        x = -0.0003713 + 1 * jax.random.normal(jax.random.fold_in(_gk, 1), (6250, 256), jnp.float32)
        _s = jax.random.randint(jax.random.fold_in(_gk, 2), (100000,), 0, 6250, jnp.int32)
        _d = jax.random.randint(jax.random.fold_in(_gk, 3), (100000,), 0, 6250, jnp.int32)
        _loop = jnp.arange(6250, dtype=jnp.int32)
        src = jnp.concatenate([_s, _d, _loop])
        dst = jnp.concatenate([_d, _s, _loop])
        _o = jnp.argsort(dst, stable=True)
        src = src[_o]
        dst = dst[_o]
        return (x, src, dst)
    x, src, dst = _rec_inputs()

    def _L0_gnn_setup():
        import jax, jax.numpy as jnp
        import numpy as np
        N = 6250
        E = 100000
        IN_DIM = 256
        HID = 64
        HEADS = 4
        NEG_SLOPE = 0.2

        def _gat_forward(x, edge_index, W, att_src, att_dst, bias):
            n = x.shape[0]
            h = (x @ W).reshape(n, HEADS, HID)
            a_src = jnp.einsum('nhf,hf->nh', h, att_src)
            a_dst = jnp.einsum('nhf,hf->nh', h, att_dst)
            loop = jnp.arange(n, dtype=edge_index.dtype)
            src = jnp.concatenate([edge_index[0], loop])
            dst = jnp.concatenate([edge_index[1], loop])
            e = jax.nn.leaky_relu(a_src[src] + a_dst[dst], NEG_SLOPE)
            m = jax.ops.segment_max(e, dst, num_segments=n)
            num = jnp.exp(e - m[dst])
            denom = jax.ops.segment_sum(num, dst, num_segments=n)
            alpha = num / denom[dst]
            msg = alpha[:, :, None] * h[src]
            out = jax.ops.segment_sum(msg, dst, num_segments=n)
            out = out.reshape(n, HEADS * HID) + bias
            return jax.nn.relu(out)
        key = jax.random.key(seed)
        k1, k2, k3, k4, k5, k6 = jax.random.split(key, 6)
        x = jax.random.normal(k1, (N, IN_DIM), dtype=jnp.float32)
        edge_index = jax.random.randint(k2, (2, E), 0, N, dtype=jnp.int64)
        W = jax.random.normal(k3, (IN_DIM, HEADS * HID), dtype=jnp.float32) / np.sqrt(IN_DIM)
        att_src = jax.random.normal(k4, (HEADS, HID), dtype=jnp.float32) / np.sqrt(HID)
        att_dst = jax.random.normal(k5, (HEADS, HID), dtype=jnp.float32) / np.sqrt(HID)
        bias = jnp.zeros((HEADS * HID,), dtype=jnp.float32)
        return {'x': x, 'edge_index': edge_index, 'W': W, 'att_src': att_src, 'att_dst': att_dst, 'bias': bias}
    _L0_gnn_all = _L0_gnn_setup()
    _L0_gnn_in = {k: v for k, v in _L0_gnn_all.items() if k in ('W', 'att_src', 'att_dst', 'bias')}
    del _L0_gnn_all

    def _L0_ffn_setup():
        import jax, jax.numpy as jnp
        import numpy as np
        C = 256
        EPS = 1e-05
        N_ITERS = 30

        def _layernorm(x, w, bias):
            mu = jnp.mean(x, axis=-1, keepdims=True)
            var = jnp.mean(jnp.square(x - mu), axis=-1, keepdims=True)
            return (x - mu) * jax.lax.rsqrt(var + EPS) * w + bias
        key = jax.random.key(seed)
        kx, kw, kb, klw, klb = jax.random.split(key, 5)
        x = jax.random.normal(kx, (8, 256, C), dtype=jnp.float32)
        bound = 1.0 / np.sqrt(C)
        W = jax.random.uniform(kw, (C, C), minval=-bound, maxval=bound, dtype=jnp.float32)
        b = jax.random.uniform(kb, (C,), minval=-bound, maxval=bound, dtype=jnp.float32)
        ln_w = jnp.ones((C,), dtype=jnp.float32)
        ln_b = jnp.zeros((C,), dtype=jnp.float32)
        return {'x': x, 'ln_w': ln_w, 'ln_b': ln_b, 'W': W, 'b': b}
    _L0_ffn_all = _L0_ffn_setup()
    _L0_ffn_in = {k: v for k, v in _L0_ffn_all.items() if k in ('ln_w', 'ln_b', 'W', 'b')}
    del _L0_ffn_all
    return {'x': x, 'src': src, 'dst': dst, 'L0_gnn_W': _L0_gnn_in['W'], 'L0_gnn_att_src': _L0_gnn_in['att_src'], 'L0_gnn_att_dst': _L0_gnn_in['att_dst'], 'L0_gnn_bias': _L0_gnn_in['bias'], 'L0_ffn_ln_w': _L0_ffn_in['ln_w'], 'L0_ffn_ln_b': _L0_ffn_in['ln_b'], 'L0_ffn_W': _L0_ffn_in['W'], 'L0_ffn_b': _L0_ffn_in['b']}

def reference(x, src, dst, L0_gnn_W, L0_gnn_att_src, L0_gnn_att_dst, L0_gnn_bias, L0_ffn_ln_w, L0_ffn_ln_b, L0_ffn_W, L0_ffn_b):
    import jax
    import jax.numpy as jnp

    def _L0_gnn_ref(x, edge_index, W, att_src, att_dst, bias):
        import jax, jax.numpy as jnp
        import numpy as np
        N = 6250
        E = 100000
        IN_DIM = 256
        HID = 64
        HEADS = 4
        NEG_SLOPE = 0.2

        def _gat_forward(x, edge_index, W, att_src, att_dst, bias):
            n = x.shape[0]
            h = (x @ W).reshape(n, HEADS, HID)
            a_src = jnp.einsum('nhf,hf->nh', h, att_src)
            a_dst = jnp.einsum('nhf,hf->nh', h, att_dst)
            loop = jnp.arange(n, dtype=edge_index.dtype)
            src = jnp.concatenate([edge_index[0], loop])
            dst = jnp.concatenate([edge_index[1], loop])
            e = jax.nn.leaky_relu(a_src[src] + a_dst[dst], NEG_SLOPE)
            m = jax.ops.segment_max(e, dst, num_segments=n)
            num = jnp.exp(e - m[dst])
            denom = jax.ops.segment_sum(num, dst, num_segments=n)
            alpha = num / denom[dst]
            msg = alpha[:, :, None] * h[src]
            out = jax.ops.segment_sum(msg, dst, num_segments=n)
            out = out.reshape(n, HEADS * HID) + bias
            return jax.nn.relu(out)
        return _gat_forward(x, edge_index, W, att_src, att_dst, bias)

    def _L0_ffn_ref(x, ln_w, ln_b, W, b):
        import jax, jax.numpy as jnp
        import numpy as np
        C = 256
        EPS = 1e-05
        N_ITERS = 30

        def _layernorm(x, w, bias):
            mu = jnp.mean(x, axis=-1, keepdims=True)
            var = jnp.mean(jnp.square(x - mu), axis=-1, keepdims=True)
            return (x - mu) * jax.lax.rsqrt(var + EPS) * w + bias

        def step(h, _):
            h = h + 0.01 * jnp.tanh(h)
            h = h * jax.nn.sigmoid(h)
            h = _layernorm(h, ln_w, ln_b)
            h = jnp.einsum('bsc,dc->bsd', h, W) + b
            return (h, None)
        x, _ = jax.lax.scan(step, x, None, length=N_ITERS)
        return x
    edge_index = jnp.stack([src, dst])
    x = x + _L0_gnn_ref(_layernorm(x, axis=-1), edge_index, L0_gnn_W, L0_gnn_att_src, L0_gnn_att_dst, L0_gnn_bias)
    x = x + _L0_ffn_ref(_layernorm(x, axis=-1)[None], L0_ffn_ln_w, L0_ffn_ln_b, L0_ffn_W, L0_ffn_b)[0]
    return x

_drawn_inputs = setup_inputs


def setup_inputs(seed=0):
    import zlib

    import numpy as np

    out = dict(_drawn_inputs(seed))
    spreads = {'L0_gnn_bias': (0.0, 0.1), 'L0_ffn_ln_w': (1.0, 0.2), 'L0_ffn_ln_b': (0.0, 0.1)}
    factors = {}
    for name, (base, spread) in spreads.items():
        noise = np.random.default_rng([zlib.crc32(name.encode()), seed]).standard_normal(out[name].shape)
        drawn = base * np.exp(spread * noise) if base else spread * noise
        out[name] = jnp.asarray(drawn.astype(out[name].dtype))
    for name, factor in factors.items():
        out[name] = (out[name] * factor).astype(out[name].dtype)
    return out
```

```python
import concourse.bass as bass
from concourse import mybir
from contextlib import ExitStack

F32 = mybir.dt.float32
I32 = mybir.dt.int32
U32 = mybir.dt.uint32
ALU = mybir.AluOpType
ACT = mybir.ActivationFunctionType
AX = mybir.AxisListType

N, C, H, HID = 6250, 256, 4, 64
E_IN = 206250
P = 128
NT = -(-N // P)
NX = NT + NT % 2
TAIL = N - (NT - 1) * P
NODES = NX * P
ZROW = NT * P
ROW = C + H

T = 8
BE = P * T
NB = -(-E_IN // BE)
EPAD = NB * BE
STEPS = NB - 1 + NT
R = 5
assert STEPS % R == 0
LAG = 3

EL = 125
assert E_IN % EL == 0
EC = E_IN // EL

NEG = -1.0e30
SLOPE = 0.2
EPS = 1e-5

ITERS = 30
CH = 2
NC = NX // CH
U = 5
assert NC % U == 0
HS = 100.0


class Chain:

    def __init__(self, eng, sem, done=0):
        self.eng, self.sem, self.base, self.n, self.reg = eng, sem, done, 0, 0

    def add(self, ins):
        self.n += 1
        return ins.then_inc(self.sem, 1)

    def wait(self):
        self.eng.wait_ge(self.sem, self.reg + (self.base + self.n))


def turns(eng, count, body, chain=None):
    start = chain.n if chain else 0
    body(0)
    if chain:
        per = chain.n - start
        chain.base, chain.n = chain.base + chain.n, 0
    with eng.Fori(1, count) as i:
        if chain:
            chain.reg = (i - 1) * per
        body(i)
    if chain:
        assert chain.n == per
        chain.base, chain.n, chain.reg = chain.base + per * (count - 1), 0, 0


def wait_count(eng, sem, count):
    if isinstance(count, int) and count <= 0:
        return
    eng.wait_ge(sem, count)


def build(nc, x, src, dst, gW, att_src, att_dst, gbias, ln_w, ln_b, fW, fb, out):
    srcp = nc.dram_tensor("srcp", (EPAD,), U32).ap()
    dstp = nc.dram_tensor("dstp", (EPAD + 8,), F32).ap()
    haug = nc.dram_tensor("haug", (NODES, ROW), F32).ap()
    anode = nc.dram_tensor("anode", (NODES, H), F32).ap()
    agg = nc.dram_tensor("agg", (NT * P, ROW), F32).ap()

    with ExitStack() as ctx:
        sb = lambda name, shape, dt=F32: ctx.enter_context(nc.sbuf_tensor(name, shape, dt))
        sem = lambda name: ctx.enter_context(nc.semaphore(name))
        res = dict(
            X=sb("X", [P, NX, C]),
            ident=sb("ident", [P, P]),
            iota_k=sb("iota_k", [P, STEPS]),
            is_last_lane=sb("is_last_lane", [P, T]),
            head_reset=sb("head_reset", [P, T]),
            half_neg=sb("half_neg", [P, NX]),
            bst=sb("bst", [P, NX, 6]),
            mv=sb("mv", [P, NX, 2]),
            ve=sb("ve", [P, NX]),
            rstd=sb("rstd", [P, NX]),
            nmr=sb("nmr", [P, NX]),
            base_k=sb("base_k", [P, STEPS]),
            first_k=sb("first_k", [P, STEPS]),
            keep_k=sb("keep_k", [P, STEPS]),
            tab_i=sb("tab_i", [1, 3, STEPS], I32),
            WT=sb("WT", [P, 2, C]),
            b100=sb("b100", [P, C]),
            gbb=sb("gbb", [P, C]),
        )
        done = prepare(nc, sem, res, x, src, dst, gW, att_src, att_dst, gbias, ln_w, ln_b, fW, fb,
                       srcp, dstp, haug, anode)
        attend(nc, sem, res, srcp, dstp, haug, anode, agg)
        scan_ffn(nc, sem, res, agg, out)


def prepare(nc, sem, res, x, src, dst, gW, att_src, att_dst, gbias, ln_w, ln_b, fW, fb,
            srcp, dstp, haug, anode):
    X, ident, iota_k, mv, rstd, nmr, ve = (res[n] for n in ("X", "ident", "iota_k", "mv", "rstd", "nmr", "ve"))
    bst, half_neg, is_last_lane, head_reset = (res[n] for n in ("bst", "half_neg", "is_last_lane", "head_reset"))
    base_k, first_k, keep_k, tab_i = (res[n] for n in ("base_k", "first_k", "keep_k", "tab_i"))
    WT, b100, gbb = res["WT"], res["b100"], res["gbb"]
    MB = NB - 1 - P
    with ExitStack() as ctx:
        sb = lambda name, shape, dt=F32: ctx.enter_context(nc.sbuf_tensor(name, shape, dt))
        pb = lambda name: ctx.enter_context(nc.psum_tensor(name, [P, 512], F32))
        ones = sb("ones", [P, P])
        iota_i = sb("iota_i", [P, STEPS], I32)
        part_i = sb("part_i", [P, 1], I32)
        part = sb("part", [P, 1])
        lane_i = sb("lane_i", [P, T], I32)
        key_i = sb("key_i", [P, 2], I32)
        key_t = sb("key_t", [P, 2], I32)
        key = sb("key", [P, 2])
        keycmp = sb("keycmp", [P, 2, STEPS])
        m_k = sb("m_k", [P, STEPS])
        d_k = sb("d_k", [P, STEPS])
        tab_f = sb("tab_f", [1, 3, STEPS])
        dst_i = sb("dst_i", [P, EC], I32)
        dst_f = sb("dst_f", [P, EC])
        padrow = sb("padrow", [1, EPAD + 8 - E_IN])
        padsrc = sb("padsrc", [1, EPAD - E_IN], U32)
        W = sb("W", [P, 2, C + 2 * H])
        attb = sb("attb", [P, 2, C])
        wprod = sb("wprod", [P, 2, 2, C])
        fWs = sb("fWs", [P, 2, C])
        fWr = sb("fWr", [P, 2, C])
        lnwb = sb("lnwb", [P, C])
        lnbb = sb("lnbb", [P, C])
        fbc = sb("fbc", [P, 2])
        rowmean = sb("rowmean", [P, 2])
        bcol = sb("bcol", [P, 2])
        bdiag = sb("bdiag", [P, 2, P])
        xn = sb("xn", [P, 2, C])
        xT = sb("xT", [P, 2, 2, P])
        hrow = sb("hrow", [P, 2, C + 2 * H])
        ps_xt = [pb(f"ps_xt{i}") for i in range(2)]
        ps_h = [pb(f"ps_h{i}") for i in range(2)]
        ps_wt = [pb(f"ps_wt{i}") for i in range(2)]
        ps_b = pb("ps_b")
        ps_mk = pb("ps_mk")

        s_in = sem("s_in")
        s_pads = sem("s_pads")
        s_iota = sem("s_iota")
        s_ones = sem("s_ones")
        s_dstf = sem("s_dstf")
        s_edges = sem("s_edges")
        s_keycmp = sem("s_keycmp")
        s_mk = sem("s_mk")
        s_tab = sem("s_tab")
        s_stats = sem("s_stats")
        s_rstd = sem("s_rstd")
        s_xn = sem("s_xn")
        s_xt = sem("s_xt")
        s_xtc = sem("s_xtc")
        s_h = sem("s_h")
        s_hrow = sem("s_hrow")
        s_hst = [sem(f"s_hst{i}") for i in range(2)]
        s_wf = sem("s_wf")
        s_wt = sem("s_wt")
        s_dprep = sem("s_dprep")
        s_pprep = sem("s_pprep")
        TURN = 2

        with nc.Block() as block:
            @block.sync
            def _(sp):
                sp.wait_ge(s_pads, 1)
                sp.dma_start(X[:, 0:NT - 1, :], x[0:(NT - 1) * P, :].rearrange("(t p) c -> p t c", p=P)).then_inc(s_in, 16)
                sp.dma_start(X[0:TAIL, NT - 1, :], x[(NT - 1) * P:N, :]).then_inc(s_in, 16)
                sp.dma_start(dst_i[0:EL, :], dst.rearrange("(p c) -> p c", c=EC)).then_inc(s_in, 16)
                sp.dma_start(srcp[0:E_IN].rearrange("(p c) -> p c", c=EC),
                             src.rearrange("(p c) -> p c", c=EC)).then_inc(s_edges, 16)
                sp.dma_start(srcp[E_IN:EPAD].rearrange("(a n) -> a n", a=1), padsrc[:, :]).then_inc(s_edges, 16)
                sp.dma_start(dstp[0:1].rearrange("(a n) -> a n", a=1), padrow[:, 0:1]).then_inc(s_edges, 16)
                sp.dma_start(dstp[E_IN + 1:EPAD + 8].rearrange("(a n) -> a n", a=1), padrow[:, 1:]).then_inc(s_edges, 16)
                sp.wait_ge(s_dstf, 1)
                sp.dma_start(dstp[1:E_IN + 1].rearrange("(p c) -> p c", c=EC), dst_f[0:EL, :]).then_inc(s_edges, 16)

                def store_rows(i):
                    for u in range(TURN):
                        sp.wait_ge(s_hrow, i * TURN + (u + 1))
                        sp.nop(nofuse=True)
                        sp.dma_start(haug[bass.ds((i * TURN + u) * P, P), :], hrow[:, u, 0:ROW]).then_inc(s_hst[u], 16)
                        sp.dma_start(anode[bass.ds((i * TURN + u) * P, P), :], hrow[:, u, ROW:ROW + H]).then_inc(s_hst[u], 16)

                turns(sp, NX // TURN, store_rows)
                for u in range(TURN):
                    sp.wait_ge(s_hst[u], 32 * (NX // TURN))
                sp.wait_ge(s_edges, 16 * 5)

            @block.scalar
            def _(act):
                act.dma_start(W[:, :, 0:C], gW.rearrange("(k p) n -> p k n", p=P)).then_inc(s_in, 16)
                act.dma_start(fWs[:, :, :], fW.rearrange("(k p) n -> p k n", p=P)).then_inc(s_in, 16)
                act.dma_start(attb[:, 0, :], att_src.rearrange("h f -> (h f)").partition_broadcast(P)).then_inc(s_in, 16)
                act.dma_start(attb[:, 1, :], att_dst.rearrange("h f -> (h f)").partition_broadcast(P)).then_inc(s_in, 16)
                act.dma_start(lnwb[:, :], ln_w.partition_broadcast(P)).then_inc(s_in, 16)
                act.dma_start(lnbb[:, :], ln_b.partition_broadcast(P)).then_inc(s_in, 16)
                act.dma_start(gbb[:, :], gbias.partition_broadcast(P)).then_inc(s_in, 16)
                with nc.allow_non_contiguous_dma(reason="single elements: a bias as a column, block ends"):
                    act.dma_start(fbc[:, :], fb.rearrange("(k p) -> p k", p=P)).then_inc(s_in, 16)
                    ends = dst[0:(NB - 1) * BE].rearrange("(m e) -> m e", e=BE)
                    act.dma_start(key_i[:, 0:1], ends[0:P, BE - 1:BE]).then_inc(s_in, 16)
                    act.dma_start(key_i[0:MB, 1:2], ends[P:NB - 1, BE - 1:BE]).then_inc(s_in, 16)
                act.wait_ge(s_rstd, 1)

                def normalise(i):
                    for u in range(TURN):
                        wait_count(act, s_xt, i * TURN + (u + 1) - TURN)
                        act.nop(nofuse=True)
                        nc.scalar.activation(xn[:, u, :], X[:, bass.ds(i * TURN + u, 1), :], ACT.Identity,
                                             scale=rstd[:, bass.ds(i * TURN + u, 1)],
                                             bias=nmr[:, bass.ds(i * TURN + u, 1)]).then_inc(s_xn, 1)

                turns(act, NX // TURN, normalise)

            @block.gpsimd
            def _(pool):
                ch = Chain(pool, s_pprep)
                nc.gpsimd.memset(X[:, NT - 1:NX, :], 0.0)
                nc.gpsimd.memset(padsrc[:, :], 0)
                ch.add(nc.gpsimd.memset(padrow[:, :], 8191.0))
                ch.wait()
                nc.gpsimd.memset(padrow[:, 0:1], -1.0).then_inc(s_pads, 1)
                nc.gpsimd.iota(iota_i[:, :], pattern=[[1, STEPS]], base=0, channel_multiplier=0)
                nc.gpsimd.iota(part_i[:, :], pattern=[[0, 1]], base=0, channel_multiplier=1)
                nc.gpsimd.iota(lane_i[:, :], pattern=[[1, T]], base=0, channel_multiplier=T).then_inc(s_iota, 1)
                nc.gpsimd.memset(ones[:, :], 1.0).then_inc(s_ones, 1)
                ch.add(nc.gpsimd.memset(half_neg[:, :], -0.5))
                ch.wait()
                pool.wait_ge(s_stats, 1)
                ch.add(nc.gpsimd.tensor_tensor(rstd[:, :], ve[:, :], half_neg[:, :], ALU.pow))
                ch.wait()
                ch.add(nc.gpsimd.tensor_tensor(nmr[:, :], rstd[:, :], mv[:, :, 0], ALU.mult))
                ch.wait()
                nc.gpsimd.tensor_scalar(nmr[:, :], nmr[:, :], -1.0, None, ALU.mult).then_inc(s_rstd, 1)

            @block.vector
            def _(dve):
                ch = Chain(dve, s_dprep)
                v = nc.vector
                dve.wait_ge(s_iota, 1)
                v.tensor_copy(iota_k[:, :], iota_i[:, :])
                v.memset(head_reset[:, :], 0.0)
                v.memset(key[:, :], 1.0e9)
                ch.add(v.tensor_copy(part[:, :], part_i[:, :]))
                ch.wait()
                v.memset(head_reset[:, 0:1], NEG)
                v.tensor_scalar(ident[:, :], iota_k[:, 0:P], part[:, :], None, ALU.is_equal)
                v.tensor_scalar(is_last_lane[:, :], lane_i[:, :], float(BE - 1), None, ALU.is_equal)
                dve.wait_ge(s_in, 16 * 13)
                v.tensor_copy(dst_f[0:EL, :], dst_i[0:EL, :]).then_inc(s_dstf, 1)
                for t in range(NX):
                    last = v.bn_stats(bst[:, t, :], X[:, t, :])
                ch.add(last)
                ch.wait()
                for t in range(NX):
                    last = v.bn_aggr(mv[:, t, :], bst[:, t, :])
                ch.add(last)
                ch.wait()
                v.tensor_scalar(ve[:, :], mv[:, :, 1], EPS, None, ALU.add).then_inc(s_stats, 1)
                v.tensor_scalar(key_t[:, 0:1], key_i[:, 0:1], 7, None, ALU.arith_shift_right)
                ch.add(v.tensor_scalar(key_t[0:MB, 1:2], key_i[0:MB, 1:2], 7, None, ALU.arith_shift_right))
                ch.wait()
                v.tensor_tensor(key[:, 0:1], key_t[:, 0:1], part[:, :], ALU.add)
                ch.add(v.scalar_tensor_tensor(out=key[0:MB, 1:2], in0=key_t[0:MB, 1:2], scalar=float(P),
                                              in1=part[0:MB, :], op0=ALU.add, op1=ALU.add))
                ch.wait()
                v.tensor_scalar(keycmp[:, 0, :], iota_k[:, :], key[:, 0:1], None, ALU.is_gt)
                v.tensor_scalar(keycmp[:, 1, :], iota_k[:, :], key[:, 1:2], None, ALU.is_gt).then_inc(s_keycmp, 1)
                for k in range(2):
                    for a in range(2):
                        last = v.tensor_tensor(wprod[:, k, a, :], W[:, k, 0:C], attb[:, a, :], ALU.mult)
                ch.add(last)
                ch.wait()
                for k in range(2):
                    for a in range(2):
                        last = v.tensor_reduce(W[:, k, C + a * H:C + (a + 1) * H],
                                               wprod[:, k, a, :].rearrange("p (h f) -> p h f", h=H),
                                               axis=AX.X, op=ALU.add)
                last.then_inc(s_wf, 1)
                dve.wait_ge(s_wf, 1)
                for k in range(2):
                    v.tensor_tensor(fWr[:, k, :], fWs[:, k, :], lnwb[:, :], ALU.mult)
                    last = v.tensor_tensor(wprod[:, k, 0, :], fWs[:, k, :], lnbb[:, :], ALU.mult)
                ch.add(last)
                ch.wait()
                v.tensor_reduce(rowmean[:, :], fWr[:, :, :], axis=AX.X, op=ALU.add)
                ch.add(v.tensor_reduce(bcol[:, :], wprod[:, :, 0, :], axis=AX.X, op=ALU.add))
                ch.wait()
                v.tensor_scalar(rowmean[:, :], rowmean[:, :], 1.0 / C, None, ALU.mult)
                ch.add(v.tensor_tensor(bcol[:, :], bcol[:, :], fbc[:, :], ALU.add))
                ch.wait()
                for k in range(2):
                    v.tensor_scalar(fWr[:, k, :], fWr[:, k, :], rowmean[:, k:k + 1], None, ALU.subtract)
                    last = v.tensor_scalar(bdiag[:, k, :], ident[:, :], bcol[:, k:k + 1], HS, ALU.mult, ALU.mult)
                last.then_inc(s_wf, 1)
                dve.wait_ge(s_mk, 1)
                ch.add(v.tensor_copy(m_k[:, :], ps_mk[:, 0:STEPS]))
                ch.wait()
                ch.add(v.tensor_tensor(d_k[:, :], iota_k[:, :], m_k[:, :], ALU.subtract))
                ch.wait()
                v.tensor_scalar(base_k[:, :], d_k[:, :], float(P), None, ALU.mult)
                v.memset(first_k[:, 0:1], 1.0)
                ch.add(v.tensor_tensor(first_k[:, 1:], d_k[:, 1:], d_k[:, 0:STEPS - 1], ALU.subtract))
                ch.wait()
                v.tensor_scalar(keep_k[:, :], first_k[:, :], -1.0, 1.0, ALU.mult, ALU.add)
                v.tensor_scalar(tab_f[:, 0, :], m_k[0:1, :], float(BE), None, ALU.mult)
                v.tensor_scalar(tab_f[:, 1, :], base_k[0:1, :], 0.0, float((NT - 1) * P), ALU.max, ALU.min)
                ch.add(v.scalar_tensor_tensor(out=tab_f[:, 2, :], in0=base_k[0:1, :], scalar=-float(ZROW),
                                              in1=first_k[0:1, :], op0=ALU.add, op1=ALU.mult))
                ch.wait()
                ch.add(v.tensor_scalar(tab_f[:, 2, :], tab_f[:, 2, :], float(ZROW), 0.0, ALU.add, ALU.max))
                ch.wait()
                ch.add(v.tensor_scalar(tab_f[:, 2, :], tab_f[:, 2, :], float(ZROW), None, ALU.min))
                ch.wait()
                v.tensor_copy(tab_i[:, :, :], tab_f[:, :, :]).then_inc(s_tab, 1)
                dve.wait_ge(s_wt, 1)
                for a in range(2):
                    v.tensor_copy(WT[:, a, :], ps_wt[a][:, 0:C])
                v.tensor_copy(b100[:, :], ps_b[:, 0:C])

                def copy_rows(i):
                    for u in range(TURN):
                        dve.wait_ge(s_xt, i * TURN + (u + 1))
                        v.tensor_copy(xT[:, u, :, :], ps_xt[u][:, 0:C].rearrange("p (k n) -> p k n", k=2)).then_inc(s_xtc, 1)
                    for u in range(TURN):
                        dve.wait_ge(s_h, i * TURN + (u + 1))
                        wait_count(dve, s_hst[u], i * 32)
                        v.tensor_copy(hrow[:, u, :], ps_h[u][:, 0:C + 2 * H]).then_inc(s_hrow, 1)

                turns(dve, NX // TURN, copy_rows)

            @block.tensor
            def _(pe):
                mm = nc.tensor.matmul
                pe.wait_ge(s_ones, 1)
                pe.wait_ge(s_keycmp, 1)
                mm(ps_mk[:, 0:STEPS], ones[:, :], keycmp[:, 0, :], start=True, stop=False)
                mm(ps_mk[:, 0:STEPS], ones[:, :], keycmp[:, 1, :], start=False, stop=True).then_inc(s_mk, 1)
                pe.wait_ge(s_wf, 2)
                for a in range(2):
                    for k in range(2):
                        nc.tensor.transpose(ps_wt[a][:, k * P:(k + 1) * P], fWr[:, k, a * P:(a + 1) * P], ident[:, :])
                for k in range(2):
                    last = mm(ps_b[:, k * P:(k + 1) * P], ones[:, :], bdiag[:, k, :], start=True, stop=True)
                last.then_inc(s_wt, 1)

                def project(i):
                    for u in range(TURN):
                        pe.wait_ge(s_xn, i * TURN + (u + 1))
                        for k in range(2):
                            last = nc.tensor.transpose(ps_xt[u][:, k * P:(k + 1) * P], xn[:, u, k * P:(k + 1) * P], ident[:, :])
                        last.then_inc(s_xt, 1)
                    for u in range(TURN):
                        pe.wait_ge(s_xtc, i * TURN + (u + 1))
                        wait_count(pe, s_hrow, i * TURN + (u + 1) - TURN)
                        for k in range(2):
                            last = mm(ps_h[u][:, 0:C + 2 * H], xT[:, u, k, :], W[:, k, :], start=(k == 0), stop=(k == 1))
                        last.then_inc(s_h, 1)

                turns(pe, NX // TURN, project)


def attend(nc, sem, res, srcp, dstp, haug, anode, agg):
    ident, iota_k, is_last_lane, head_reset = (res[n] for n in ("ident", "iota_k", "is_last_lane", "head_reset"))
    base_k, first_k, keep_k, tab_i = (res[n] for n in ("base_k", "first_k", "keep_k", "tab_i"))
    with ExitStack() as ctx:
        sb = lambda name, shape, dt=F32: ctx.enter_context(nc.sbuf_tensor(name, shape, dt))
        pb = lambda name: ctx.enter_context(nc.psum_tensor(name, [P, 512], F32))
        idx = sb("idx", [P, R, T], U32)
        dw = sb("dw", [P, R, T + 2])
        selfr = sb("selfr", [P, R, ROW])
        an = sb("an", [P, R, H])
        G = sb("G", [P, R, T, ROW])
        acc = sb("acc", [P, R, ROW])
        neq = sb("neq", [P, T + 1])
        ff = sb("ff", [P, T])
        tr = sb("tr", [P, 2 * H])
        rel = sb("rel", [P, T])
        fadd = sb("fadd", [P, H, T])
        onehot = sb("onehot", [P, T, P])
        onehotT = sb("onehotT", [P, T, P])
        sv = sb("sv", [P, H, T])
        seg = sb("seg", [P, H, T])
        ffT = sb("ffT", [H, P])
        run = sb("run", [H, P + 1])
        ent = sb("ent", [P, H, T])
        full = sb("full", [P, H, T])
        lastmax = sb("lastmax", [P, T, H + 1])
        absent = sb("absent", [P, 1])
        mx = sb("mx", [P, 2, H])
        zz = sb("zz", [P, 2, H])
        nodev = sb("nodev", [P, 3, H])
        dal = sb("dal", [P, H])
        alpha = sb("alpha", [P, H])
        scaled = sb("scaled", [P, ROW])
        ez = sb("ez", [P, T, H])
        el = sb("el", [P, T, H])
        ps_ot = [pb(f"ps_ot{i}") for i in range(2)]
        ps_tr = pb("ps_tr")
        ps_in = pb("ps_in")
        ps_mn = pb("ps_mn")
        ps_ex = pb("ps_ex")
        ps_sum = [pb(f"ps_sum{i}") for i in range(2)]
        TH = T // 2

        LOADS = 5
        s_ld = [sem(f"s_ld{u}") for u in range(R)]
        s_g = [sem(f"s_g{u}") for u in range(R)]
        s_st = [sem(f"s_st{u}") for u in range(R)]
        s_onehot = sem("s_onehot")
        s_ot = sem("s_ot")
        s_otc = sem("s_otc")
        s_tr = sem("s_tr")
        s_trT = sem("s_trT")
        s_ffT = sem("s_ffT")
        s_run = sem("s_run")
        s_enter = sem("s_enter")
        s_lastmax = sem("s_lastmax")
        s_mn = sem("s_mn")
        s_nodev = sem("s_nodev")
        s_ex = sem("s_ex")
        s_dal = sem("s_dal")
        s_alpha = sem("s_alpha")
        s_el = sem("s_el")
        s_w = sem("s_w")
        s_msg = sem("s_msg")
        s_sum = sem("s_sum")
        s_acc = sem("s_acc")
        s_datt = sem("s_datt")
        s_patt = sem("s_patt")
        TURNS = STEPS // R

        with nc.Block() as block:
            @block.sync
            def _(sp):
                def load(i, u):
                    k = i * R + u
                    wait_count(sp, s_acc, k + 1 - R)
                    sp.nop(nofuse=True)
                    eb = sp.value_load(tab_i[0:1, 0, bass.ds(k, 1)], min_val=0, max_val=EPAD - BE)
                    nb = sp.value_load(tab_i[0:1, 1, bass.ds(k, 1)], min_val=0, max_val=(NT - 1) * P)
                    zb = sp.value_load(tab_i[0:1, 2, bass.ds(k, 1)], min_val=0, max_val=ZROW)
                    sp.dma_start(idx[:, u, :], srcp[bass.ds(eb, BE)].rearrange("(p t) -> p t", t=T)).then_inc(s_ld[u], 16)
                    sp.dma_start(dw[:, u, 0:T], dstp[bass.ds(eb, BE)].rearrange("(p t) -> p t", t=T)).then_inc(s_ld[u], 16)
                    sp.dma_start(dw[:, u, T:T + 2],
                                 dstp[bass.ds(eb + T, BE)].rearrange("(p t) -> p t", t=T)[:, 0:2]).then_inc(s_ld[u], 16)
                    sp.dma_start(selfr[:, u, :], haug[bass.ds(zb, P), :]).then_inc(s_ld[u], 16)
                    sp.dma_start(an[:, u, :], anode[bass.ds(nb, P), :]).then_inc(s_ld[u], 16)

                def store(i, u):
                    k = i * R + u
                    sp.wait_ge(s_acc, k + 1)
                    sp.nop(nofuse=True)
                    if u:
                        sp.wait_ge(s_st[u - 1], (i + 1) * 16)
                    else:
                        wait_count(sp, s_st[R - 1], i * 16)
                    sp.nop(nofuse=True)
                    nb = sp.value_load(tab_i[0:1, 1, bass.ds(k, 1)], min_val=0, max_val=(NT - 1) * P)
                    sp.dma_start(agg[bass.ds(nb, P), :], acc[:, u, :]).then_inc(s_st[u], 16)

                def traffic(i):
                    for u in range(R):
                        load(i, u)
                        if u >= LAG:
                            store(i, u - LAG)
                        elif not isinstance(i, int):
                            store(i - 1, u - LAG + R)

                turns(sp, TURNS, traffic)
                for u in range(R - LAG, R):
                    store(TURNS - 1, u)
                for u in range(R):
                    sp.wait_ge(s_st[u], TURNS * 16)

            @block.gpsimd
            def _(pool):
                def gather(i):
                    for u in range(R):
                        pool.wait_ge(s_ld[u], (i + 1) * (16 * LOADS))
                        pool.nop(nofuse=True)
                        for t in range(T):
                            pool.indirect_dma_start(
                                out=G[:, u, t, :], out_offset=None, in_=haug[:, :],
                                in_offset=bass.IndirectOffsetOnAxis(ap=idx[:, u, t:t + 1], axis=0),
                            ).then_inc(s_g[u], 16)

                turns(pool, TURNS, gather)

            @block.scalar
            def _(act):
                def weights(i):
                    for u in range(R):
                        k = i * R + u
                        act.wait_ge(s_ot, k + 1)
                        for b in range(2):
                            last = nc.scalar.activation(onehotT[:, b * TH:(b + 1) * TH, :],
                                                        ps_ot[b][:, :].rearrange("p (t e) -> p t e", e=P), ACT.Copy)
                        last.then_inc(s_otc, 1)
                        act.wait_ge(s_trT, k + 1)
                        nc.scalar.activation(ffT[:, :], ps_tr[0:H, P:2 * P], ACT.Copy).then_inc(s_ffT, 1)
                        act.wait_ge(s_dal, k + 1)
                        nc.scalar.activation(alpha[:, :], dal[:, :], ACT.Exp).then_inc(s_alpha, 1)
                        act.wait_ge(s_el, k + 1)
                        nc.scalar.activation(G[:, u, :, C:ROW], el[:, :, :], ACT.Exp).then_inc(s_w, 1)

                turns(act, TURNS, weights)

            @block.vector
            def _(dve):
                ch = Chain(dve, s_datt)
                v = nc.vector
                v.memset(run[:, :], NEG)
                v.memset(mx[:, :, :], 0.0)
                ch.add(v.memset(acc[:, R - 1, :], 0.0))
                ch.wait()

                def step(i):
                    for u in range(R):
                        k = i * R + u
                        col = bass.ds(k, 1)
                        prev = (u - 1) % R
                        dve.wait_ge(s_ld[u], (i + 1) * (16 * LOADS))
                        v.tensor_tensor(neq[:, :], dw[:, u, 1:T + 2], dw[:, u, 0:T + 1], ALU.not_equal)
                        v.tensor_scalar(ff[:, :], dw[:, u, 1:T + 1], dw[:, u, 0:1], NEG, ALU.not_equal, ALU.mult)
                        v.tensor_scalar(tr[:, H:2 * H], dw[:, u, T:T + 1].to_broadcast([P, H]), dw[:, u, 0:1], NEG,
                                        ALU.not_equal, ALU.mult)
                        v.tensor_scalar(rel[:, :], dw[:, u, 1:T + 1], base_k[:, col], None, ALU.subtract)
                        v.tensor_copy(nodev[:, 2, :], an[:, u, :])
                        v.scalar_tensor_tensor(out=mx[:, 0, :], in0=mx[:, 1, :], scalar=keep_k[:, col],
                                               in1=selfr[:, u, C:ROW], op0=ALU.mult, op1=ALU.add)
                        v.scalar_tensor_tensor(out=scaled[:, 0:C], in0=acc[:, prev, 0:C], scalar=keep_k[:, col],
                                               in1=selfr[:, u, 0:C], op0=ALU.mult, op1=ALU.add)
                        ch.add(v.tensor_scalar(scaled[:, C:ROW], acc[:, prev, C:ROW], keep_k[:, col],
                                               first_k[:, col], ALU.mult, ALU.add))
                        ch.wait()
                        v.scalar_tensor_tensor(out=fadd[:, :, :], in0=neq[:, 0:T].unsqueeze(1).to_broadcast([P, H, T]),
                                               scalar=NEG, in1=head_reset[:, :].unsqueeze(1).to_broadcast([P, H, T]),
                                               op0=ALU.mult, op1=ALU.add)
                        v.tensor_tensor(lastmax[:, :, H], neq[:, 1:T + 1], is_last_lane[:, :], ALU.max)
                        v.tensor_tensor(onehot[:, :, :], rel[:, :].unsqueeze(2).to_broadcast([P, T, P]),
                                        iota_k[:, 0:P].unsqueeze(1).to_broadcast([P, T, P]),
                                        ALU.is_equal).then_inc(s_onehot, 1)
                        dve.wait_ge(s_g[u], (i + 1) * (16 * T))
                        ch.add(v.tensor_copy(sv[:, :, :], G[:, u, :, C:ROW].rearrange("p t h -> p h t")))
                        ch.wait()
                        ch.add(v.tensor_tensor_scan(seg[:, :, :].rearrange("p h t -> p (h t)"),
                                                    fadd[:, :, :].rearrange("p h t -> p (h t)"),
                                                    sv[:, :, :].rearrange("p h t -> p (h t)"), NEG, ALU.add, ALU.max))
                        ch.wait()
                        v.tensor_copy(tr[:, 0:H], seg[:, :, T - 1]).then_inc(s_tr, 1)
                        dve.wait_ge(s_ffT, k + 1)
                        v.tensor_tensor_scan(run[:, 1:P + 1], ffT[:, :], ps_tr[0:H, 0:P], NEG,
                                             ALU.add, ALU.max).then_inc(s_run, 1)
                        dve.wait_ge(s_enter, k + 1)
                        ch.add(v.tensor_tensor(ent[:, :, :], ff[:, :].unsqueeze(1).to_broadcast([P, H, T]),
                                               ps_in[:, 0:H].unsqueeze(2).to_broadcast([P, H, T]), ALU.add))
                        ch.wait()
                        ch.add(v.tensor_tensor(full[:, :, :], seg[:, :, :], ent[:, :, :], ALU.max))
                        ch.wait()
                        v.tensor_tensor(lastmax[:, :, 0:H], full[:, :, :].rearrange("p h t -> p t h"),
                                        lastmax[:, :, H].unsqueeze(2).to_broadcast([P, T, H]),
                                        ALU.mult).then_inc(s_lastmax, 1)
                        dve.wait_ge(s_mn, k + 1)
                        ch.add(v.tensor_scalar(absent[:, :], ps_mn[:, H:H + 1], -1.0, -NEG, ALU.add, ALU.mult))
                        ch.wait()
                        ch.add(v.scalar_tensor_tensor(out=mx[:, 1, :], in0=ps_mn[:, 0:H], scalar=absent[:, :],
                                                      in1=mx[:, 0, :], op0=ALU.add, op1=ALU.max))
                        ch.wait()
                        ch.add(v.tensor_tensor(zz[:, :, :], mx[:, :, :],
                                               nodev[:, 2, :].unsqueeze(1).to_broadcast([P, 2, H]), ALU.add))
                        ch.wait()
                        v.scalar_tensor_tensor(out=nodev[:, 0:2, :], in0=zz[:, :, :], scalar=SLOPE, in1=zz[:, :, :],
                                               op0=ALU.mult, op1=ALU.max).then_inc(s_nodev, 1)
                        dve.wait_ge(s_nodev, k + 1)
                        v.tensor_tensor(dal[:, :], nodev[:, 0, :], nodev[:, 1, :], ALU.subtract).then_inc(s_dal, 1)
                        dve.wait_ge(s_alpha, k + 1)
                        v.tensor_tensor(scaled[:, 0:C].rearrange("p (h f) -> p h f", h=H),
                                        scaled[:, 0:C].rearrange("p (h f) -> p h f", h=H),
                                        alpha[:, :].unsqueeze(2).to_broadcast([P, H, HID]), ALU.mult)
                        ch.add(v.tensor_tensor(scaled[:, C:ROW], scaled[:, C:ROW], alpha[:, :], ALU.mult))
                        dve.wait_ge(s_ex, k + 1)
                        exv = ps_ex[:, 0:T * 2 * H].rearrange("p (t j h) -> p t j h", t=T, j=2)
                        ch.add(v.tensor_tensor(ez[:, :, :], G[:, u, :, C:ROW], exv[:, :, 1, :], ALU.add))
                        ch.wait()
                        ch.add(v.scalar_tensor_tensor(out=el[:, :, :], in0=ez[:, :, :], scalar=SLOPE, in1=ez[:, :, :],
                                                      op0=ALU.mult, op1=ALU.max))
                        ch.wait()
                        ch.add(v.tensor_tensor(ez[:, :, :], el[:, :, :], exv[:, :, 0, :], ALU.subtract))
                        ch.wait()
                        v.tensor_scalar(el[:, :, :], ez[:, :, :], 0.0, None, ALU.min).then_inc(s_el, 1)
                        dve.wait_ge(s_w, k + 1)
                        for b in range(2):
                            gh = G[:, u, b * TH:(b + 1) * TH, 0:C].rearrange("p t (h f) -> p t h f", h=H)
                            v.tensor_tensor(gh, gh, G[:, u, b * TH:(b + 1) * TH, C:ROW].unsqueeze(3)
                                            .to_broadcast([P, TH, H, HID]), ALU.mult).then_inc(s_msg, 1)
                        dve.wait_ge(s_sum, k + 1)
                        wait_count(dve, s_st[u], i * 16)
                        v.tensor_tensor(acc[:, u, :], scaled[:, :], ps_sum[u % 2][:, 0:ROW], ALU.add).then_inc(s_acc, 1)
                        dve.wait_ge(s_acc, k + 1)

                turns(dve, TURNS, step, ch)

            @block.tensor
            def _(pe):
                mm, xp = nc.tensor.matmul, nc.tensor.transpose

                def products(i):
                    for u in range(R):
                        k = i * R + u
                        pe.wait_ge(s_onehot, k + 1)
                        for t in range(T):
                            last = xp(ps_ot[t // TH][:, (t % TH) * P:(t % TH + 1) * P], onehot[:, t, :], ident[:, :])
                        last.then_inc(s_ot, 1)
                        pe.wait_ge(s_tr, k + 1)
                        xp(ps_tr[0:H, 0:P], tr[:, 0:H], ident[:, :])
                        xp(ps_tr[0:H, P:2 * P], tr[:, H:2 * H], ident[:, :]).then_inc(s_trT, 1)
                        pe.wait_ge(s_run, k + 1)
                        mm(ps_in[:, 0:H], run[:, 0:P], ident[0:H, 0:H], start=True, stop=True).then_inc(s_enter, 1)
                        pe.wait_ge(s_lastmax, k + 1)
                        for t in range(T):
                            last = mm(ps_mn[:, 0:H + 1], onehot[:, t, :], lastmax[:, t, :], start=(t == 0), stop=(t == T - 1))
                        last.then_inc(s_mn, 1)
                        pe.wait_ge(s_otc, k + 1)
                        pe.wait_ge(s_nodev, k + 1)
                        for t in range(T):
                            last = mm(ps_ex[:, t * 2 * H:(t + 1) * 2 * H], onehotT[:, t, :],
                                      nodev[:, 1:3, :].rearrange("p j h -> p (j h)"), start=True, stop=True)
                        last.then_inc(s_ex, 1)
                        for t in range(T):
                            if t % TH == 0:
                                pe.wait_ge(s_msg, 2 * k + (t // TH + 1))
                            last = mm(ps_sum[u % 2][:, 0:ROW], onehot[:, t, :], G[:, u, t, :], start=(t == 0), stop=(t == T - 1))
                        last.then_inc(s_sum, 1)

                turns(pe, TURNS, products)


def scan_ffn(nc, sem, res, agg, out):
    X, ident, mv, rstd, nmr, ve, bst, half_neg = (res[n] for n in ("X", "ident", "mv", "rstd", "nmr", "ve", "bst", "half_neg"))
    WT, b100, gbb = res["WT"], res["b100"], res["gbb"]
    QT = 7
    assert NT % QT == 0
    with ExitStack() as ctx:
        sb = lambda name, shape, dt=F32: ctx.enter_context(nc.sbuf_tensor(name, shape, dt))
        pb = lambda name: ctx.enter_context(nc.psum_tensor(name, [P, 512], F32))
        Hs = sb("Hs", [P, NX, C])
        den = sb("den", [P, NT, H])
        rden = sb("rden", [P, NT, H])
        th = sb("th", [P, U, CH * C])
        h1 = sb("h1", [P, U, CH * C])
        h2 = sb("h2", [P, U, CH * C])
        h2T = sb("h2T", [P, U, CH * C])
        cst = sb("cst", [P, U, CH, 6])
        cmv = sb("cmv", [P, U, CH, 2])
        cve = sb("cve", [P, U, CH])
        r100 = sb("r100", [P, U, CH])
        ps_x = [pb(f"ps_x{i}") for i in range(3)]
        ps_g = [pb(f"ps_g{i}") for i in range(U)]
        XB = [0, 1, 2, 0, 1]
        XD = [2, 2, 5, 3, 3]
        s_agg = sem("s_aggin")
        s_den = sem("s_den")
        s_x1var = sem("s_x1var")
        s_x1root = sem("s_x1root")
        s_aff = sem("s_aff")
        s_tanh = sem("s_tanh")
        s_add = sem("s_add")
        s_silu = sem("s_silu")
        s_ve = sem("s_ve")
        s_r = sem("s_r")
        s_xp = sem("s_xp")
        s_h2T = sem("s_h2T")
        s_prod = sem("s_prod")
        s_dffn = sem("s_dffn")
        s_bn = sem("s_bn")
        s_pffn = sem("s_pffn")
        s_fin = sem("s_fin")
        s_out = sem("s_out")
        TURNS = NC // U
        ALL = ITERS * NC

        def chunk_rows(ap, j):
            return ap[:, bass.ds(j * CH, CH), :].rearrange("p a c -> p (a c)")

        def iterate(eng, turn):
            turn(0, 0)
            turn(U, U)
            with eng.Fori(2, TURNS) as b:
                turn(b * U, b * U)
            with eng.Fori(1, ITERS) as it:
                with eng.Fori(0, TURNS) as b:
                    turn(it * NC + b * U, b * U)

        with nc.Block() as block:
            @block.sync
            def _(sp):
                for b in range(NT // QT):
                    rows = agg[b * QT * P:(b + 1) * QT * P, :]
                    sp.dma_start(Hs[:, b * QT:(b + 1) * QT, :], rows[:, 0:C].rearrange("(t p) c -> p t c", p=P)).then_inc(s_agg, 16)
                sp.dma_start(den[:, :, :], agg[:, C:ROW].rearrange("(t p) h -> p t h", p=P)).then_inc(s_den, 16)
                sp.wait_ge(s_fin, 1)
                sp.dma_start(out[0:(NT - 1) * P, :].rearrange("(t p) c -> p t c", p=P), X[:, 0:NT - 1, :]).then_inc(s_out, 16)
                sp.dma_start(out[(NT - 1) * P:N, :], X[0:TAIL, NT - 1, :]).then_inc(s_out, 16)
                sp.wait_ge(s_out, 32)

            @block.gpsimd
            def _(pool):
                ch = Chain(pool, s_pffn)
                pool.wait_ge(s_x1var, 1)
                ch.add(nc.gpsimd.tensor_tensor(rstd[:, :], ve[:, :], half_neg[:, :], ALU.pow))
                ch.wait()
                nc.gpsimd.tensor_tensor(nmr[:, :], rstd[:, :], mv[:, :, 0], ALU.mult).then_inc(s_x1root, 1)

                def turn(q0, j0):
                    for u in range(U):
                        q = q0 + u
                        pool.wait_ge(s_tanh, q + 1)
                        wait_count(pool, s_silu, q + 1 - U)
                        pool.nop(nofuse=True)
                        nc.gpsimd.tensor_tensor(h1[:, u, :], chunk_rows(Hs, j0 + u), th[:, u, :], ALU.add).then_inc(s_add, 1)
                        if not (isinstance(q, int) and q < 3):
                            root(q - 3, (u - 3) % U)

                def root(q, u):
                    pool.wait_ge(s_ve, q + 1)
                    pool.wait_ge(s_aff, q + (NC + 1 - U))
                    nc.gpsimd.tensor_tensor(r100[:, u, :], cve[:, u, :], half_neg[:, 0:CH], ALU.pow).then_inc(s_r, 1)

                iterate(pool, turn)
                for q in range(ALL - 3, ALL):
                    root(q, q % U)

            @block.scalar
            def _(act):
                def silu(q, u):
                    act.wait_ge(s_add, q + 1)
                    wait_count(act, s_xp, q + 1 - U)
                    wait_count(act, s_ve, q + 1 - U)
                    nc.scalar.activation(h2[:, u, :], h1[:, u, :], ACT.Silu, scale=1.0 / HS).then_inc(s_silu, 1)

                def copy_t(q, u):
                    act.wait_ge(s_xp, q + 1)
                    wait_count(act, s_prod, q + 1 - U)
                    nc.scalar.activation(h2T[:, u, :], ps_x[XB[u]][:, :], ACT.Copy).then_inc(s_h2T, 1)

                def turn(q0, j0):
                    for u in range(U):
                        q = q0 + u
                        act.wait_ge(s_aff, q + 1)
                        wait_count(act, s_add, q + 1 - U)
                        act.nop(nofuse=True)
                        nc.scalar.activation(th[:, u, :], chunk_rows(Hs, j0 + u), ACT.Tanh, scale=1.0 / HS).then_inc(s_tanh, 1)
                        if not (isinstance(q, int) and q < 1):
                            silu(q - 1, (u - 1) % U)
                        if not (isinstance(q, int) and q < 3):
                            copy_t(q - 3, (u - 3) % U)

                iterate(act, turn)
                silu(ALL - 1, (ALL - 1) % U)
                for q in range(ALL - 3, ALL):
                    copy_t(q, q % U)

            @block.vector
            def _(dve):
                ch = Chain(dve, s_dffn)
                v = nc.vector
                v.memset(Hs[:, NT:NX, :], 0.0)
                dve.wait_ge(s_den, 16)
                ch.add(v.reciprocal(rden[:, :, :], den[:, :, :]))
                ch.wait()
                dve.wait_ge(s_agg, 16 * (NT // QT))
                for b in range(NT // QT):
                    hs = Hs[:, b * QT:(b + 1) * QT, :].rearrange("p t (h f) -> p (t h) f", h=H)
                    rd = rden[:, b * QT:(b + 1) * QT, :].rearrange("p t h -> p (t h)").unsqueeze(2)
                    ch.add(v.tensor_tensor(hs, hs, rd.to_broadcast([P, QT * H, HID]), ALU.mult))
                ch.wait()
                for b in range(NT // QT):
                    hs = Hs[:, b * QT:(b + 1) * QT, :]
                    ch.add(v.tensor_tensor(hs, hs, gbb[:, :].unsqueeze(1).to_broadcast([P, QT, C]), ALU.add))
                ch.wait()
                for b in range(NT // QT):
                    xs = X[:, b * QT:(b + 1) * QT, :].rearrange("p t c -> p (t c)")
                    hs = Hs[:, b * QT:(b + 1) * QT, :].rearrange("p t c -> p (t c)")
                    ch.add(v.scalar_tensor_tensor(out=xs, in0=hs, scalar=0.0, in1=xs, op0=ALU.max, op1=ALU.add))
                ch.wait()
                for t in range(NX):
                    last = v.bn_stats(bst[:, t, :], X[:, t, :])
                ch.add(last)
                ch.wait()
                for t in range(NX):
                    last = v.bn_aggr(mv[:, t, :], bst[:, t, :])
                ch.add(last)
                ch.wait()
                v.tensor_scalar(ve[:, :], mv[:, :, 1], EPS, None, ALU.add).then_inc(s_x1var, 1)
                dve.wait_ge(s_x1root, 1)
                v.tensor_scalar(nmr[:, :], nmr[:, :], -HS, None, ALU.mult)
                ch.add(v.tensor_scalar(rstd[:, :], rstd[:, :], HS, None, ALU.mult))
                ch.wait()
                for j in range(NC):
                    for a in range(CH):
                        t = j * CH + a
                        last = v.tensor_scalar(Hs[:, t, :], X[:, t, :], rstd[:, t:t + 1], nmr[:, t:t + 1], ALU.mult, ALU.add)
                    last.then_inc(s_aff, 1)

                def stats(q, u):
                    dve.wait_ge(s_silu, q + 1)
                    for a in range(CH):
                        last = v.bn_stats(cst[:, u, a, :], h2[:, u, a * C:(a + 1) * C])
                    last.then_inc(s_bn, 1)
                    dve.wait_ge(s_bn, 2 * q + 1)
                    dve.nop(nofuse=True)
                    for a in range(CH):
                        last = v.bn_aggr(cmv[:, u, a, :], cst[:, u, a, :])
                    last.then_inc(s_bn, 1)
                    dve.wait_ge(s_bn, 2 * q + 2)
                    wait_count(dve, s_r, q + 1 - U)
                    v.tensor_scalar(cve[:, u, :], cmv[:, u, :, 1], EPS, 1.0 / (HS * HS), ALU.add, ALU.mult).then_inc(s_ve, 1)

                def affine(q, j, u):
                    dve.wait_ge(s_prod, q + 1)
                    dve.wait_ge(s_r, q + 1)
                    for a in range(CH):
                        last = v.scalar_tensor_tensor(out=Hs[:, bass.ds(j * CH + a, 1), :].rearrange("p a c -> p (a c)"),
                                                      in0=ps_g[u][:, a * C:(a + 1) * C],
                                                      scalar=r100[:, u, a:a + 1], in1=b100[:, :], op0=ALU.mult, op1=ALU.add)
                    last.then_inc(s_aff, 1)

                LEAD = 3
                for q in range(LEAD):
                    stats(q, q)

                def turn(q0, j0, lead=U):
                    for u in range(U):
                        if u < lead:
                            stats(q0 + (u + LEAD), (u + LEAD) % U)
                        affine(q0 + u, j0 + u, u)

                turn(0, 0)
                with dve.Fori(1, TURNS) as b:
                    turn(b * U, b * U)
                with dve.Fori(1, ITERS - 1) as it:
                    with dve.Fori(0, TURNS) as b:
                        turn(it * NC + b * U, b * U)
                with dve.Fori(0, TURNS - 1) as b:
                    turn(b * U + (ITERS - 1) * NC, b * U)
                turn(ALL - U, NC - U, lead=U - LEAD)
                dve.wait_ge(s_aff, NC + ALL)
                for b in range(NT // QT):
                    xs = X[:, b * QT:(b + 1) * QT, :].rearrange("p t c -> p (t c)")
                    hs = Hs[:, b * QT:(b + 1) * QT, :].rearrange("p t c -> p (t c)")
                    last = v.scalar_tensor_tensor(out=xs, in0=hs, scalar=1.0 / HS, in1=xs, op0=ALU.mult, op1=ALU.add)
                last.then_inc(s_fin, 1)

            @block.tensor
            def _(pe):
                def transposes(q, u):
                    pe.wait_ge(s_silu, q + 1)
                    wait_count(pe, s_h2T, q + 1 - XD[u])
                    for n in range(CH * 2):
                        last = nc.tensor.transpose(ps_x[XB[u]][:, n * P:(n + 1) * P], h2[:, u, n * P:(n + 1) * P], ident[:, :])
                    last.then_inc(s_xp, 1)

                def product(q, u):
                    pe.wait_ge(s_h2T, q + 1)
                    pe.wait_ge(s_aff, q + (NC + 1 - U))
                    for a in range(CH):
                        for k in range(2):
                            last = nc.tensor.matmul(ps_g[u][:, a * C:(a + 1) * C], h2T[:, u, (a * 2 + k) * P:(a * 2 + k + 1) * P],
                                                    WT[:, k, :], start=(k == 0), stop=(k == 1))
                    last.then_inc(s_prod, 1)

                def turn(q0, j0):
                    for u in range(U):
                        q = q0 + u
                        transposes(q, u)
                        if not (isinstance(q, int) and q < 2):
                            product(q - 2, (u - 2) % U)

                iterate(pe, turn)
                for q in range(ALL - 2, ALL):
                    product(q, q % U)


def kernel(x, src, dst, L0_gnn_W, L0_gnn_att_src, L0_gnn_att_dst, L0_gnn_bias,
           L0_ffn_ln_w, L0_ffn_ln_b, L0_ffn_W, L0_ffn_b):
    import numpy as np
    import concourse.bacc as bacc
    from concourse.bass_utils import run_bass_kernel_spmd

    arrays = {
        "x": x, "src": src, "dst": dst, "gnn_W": L0_gnn_W, "att_src": L0_gnn_att_src,
        "att_dst": L0_gnn_att_dst, "gnn_bias": L0_gnn_bias, "ln_w": L0_ffn_ln_w, "ln_b": L0_ffn_ln_b,
        "ffn_W": L0_ffn_W, "ffn_b": L0_ffn_b,
    }
    arrays = {n: np.ascontiguousarray(a) for n, a in arrays.items()}
    arrays["src"] = arrays["src"].view(np.uint32)
    nc = bacc.Bacc("TRN2", target_bir_lowering=False, num_devices=1)
    args = [nc.dram_tensor(n, a.shape, mybir.dt.from_np(a.dtype), kind="ExternalInput").ap() for n, a in arrays.items()]
    out = nc.dram_tensor("out", (N, C), F32, kind="ExternalOutput").ap()
    build(nc, *args, out)
    return run_bass_kernel_spmd(nc, [arrays], core_ids=[0]).results[0]["out"]
```

```python
import concourse.bass as bass
from concourse import mybir
from contextlib import ExitStack

F32 = mybir.dt.float32
I32 = mybir.dt.int32
U32 = mybir.dt.uint32
ALU = mybir.AluOpType
ACT = mybir.ActivationFunctionType
AX = mybir.AxisListType

N, C, H, HID = 6250, 256, 4, 64
E_IN = 206250
P = 128
NT = -(-N // P)
NX = NT + NT % 2
TAIL = N - (NT - 1) * P
NODES = NX * P
ZROW = NT * P
ROW = C + H

T = 8
BE = P * T
NB = -(-E_IN // BE)
EPAD = NB * BE
STEPS = NB - 1 + NT
R = 5
assert STEPS % R == 0
LAG = R

EL = 125
assert E_IN % EL == 0
EC = E_IN // EL

NEG = -1.0e30
SLOPE = 0.2
EPS = 1e-5

ITERS = 30
CH = 2
NC = NX // CH
U = 5
assert NC % U == 0
HS = 100.0


class Chain:

    def __init__(self, eng, sem, done=0):
        self.eng, self.sem, self.base, self.n, self.reg = eng, sem, done, 0, 0

    def add(self, ins):
        self.n += 1
        return ins.then_inc(self.sem, 1)

    def wait(self):
        self.eng.wait_ge(self.sem, self.reg + (self.base + self.n))


def turns(eng, count, body, chain=None, written=1):
    for i in range(written):
        start = chain.n if chain else 0
        body(i)
    if chain:
        per = chain.n - start
        chain.base, chain.n = chain.base + chain.n, 0
    with eng.Fori(written, count) as i:
        if chain:
            chain.reg = (i - written) * per
        body(i)
    if chain:
        assert chain.n == per
        chain.base, chain.n, chain.reg = chain.base + per * (count - written), 0, 0


def wait_count(eng, sem, count):
    if isinstance(count, int) and count <= 0:
        return
    eng.wait_ge(sem, count)


def build(nc, x, src, dst, gW, att_src, att_dst, gbias, ln_w, ln_b, fW, fb, out):
    srcp = nc.dram_tensor("srcp", (EPAD,), U32).ap()
    dstp = nc.dram_tensor("dstp", (EPAD + 8,), F32).ap()
    haug = nc.dram_tensor("haug", (NODES, ROW), F32).ap()
    anode = nc.dram_tensor("anode", (NODES, H), F32).ap()
    agg = nc.dram_tensor("agg", (NT * P, ROW), F32).ap()

    with ExitStack() as ctx:
        sb = lambda name, shape, dt=F32: ctx.enter_context(nc.sbuf_tensor(name, shape, dt))
        sem = lambda name: ctx.enter_context(nc.semaphore(name))
        res = dict(
            X=sb("X", [P, NX, C]),
            ident=sb("ident", [P, P]),
            iota_k=sb("iota_k", [P, STEPS]),
            is_last_lane=sb("is_last_lane", [P, T]),
            head_reset=sb("head_reset", [P, T]),
            half_neg=sb("half_neg", [P, NX]),
            bst=sb("bst", [P, NX, 6]),
            mv=sb("mv", [P, NX, 2]),
            ve=sb("ve", [P, NX]),
            rstd=sb("rstd", [P, NX]),
            nmr=sb("nmr", [P, NX]),
            base_k=sb("base_k", [P, STEPS]),
            first_k=sb("first_k", [P, STEPS]),
            keep_k=sb("keep_k", [P, STEPS]),
            tab_i=sb("tab_i", [1, 3, STEPS], I32),
            WT=sb("WT", [P, 2, C]),
            b100=sb("b100", [P, C]),
            gbb=sb("gbb", [P, C]),
        )
        done = prepare(nc, sem, res, x, src, dst, gW, att_src, att_dst, gbias, ln_w, ln_b, fW, fb,
                       srcp, dstp, haug, anode)
        attend(nc, sem, res, srcp, dstp, haug, anode, agg)
        scan_ffn(nc, sem, res, agg, out)


def prepare(nc, sem, res, x, src, dst, gW, att_src, att_dst, gbias, ln_w, ln_b, fW, fb,
            srcp, dstp, haug, anode):
    X, ident, iota_k, mv, rstd, nmr, ve = (res[n] for n in ("X", "ident", "iota_k", "mv", "rstd", "nmr", "ve"))
    bst, half_neg, is_last_lane, head_reset = (res[n] for n in ("bst", "half_neg", "is_last_lane", "head_reset"))
    base_k, first_k, keep_k, tab_i = (res[n] for n in ("base_k", "first_k", "keep_k", "tab_i"))
    WT, b100, gbb = res["WT"], res["b100"], res["gbb"]
    MB = NB - 1 - P
    with ExitStack() as ctx:
        sb = lambda name, shape, dt=F32: ctx.enter_context(nc.sbuf_tensor(name, shape, dt))
        pb = lambda name: ctx.enter_context(nc.psum_tensor(name, [P, 512], F32))
        ones = sb("ones", [P, P])
        iota_i = sb("iota_i", [P, STEPS], I32)
        part_i = sb("part_i", [P, 1], I32)
        part = sb("part", [P, 1])
        lane_i = sb("lane_i", [P, T], I32)
        key_i = sb("key_i", [P, 2], I32)
        key_t = sb("key_t", [P, 2], I32)
        key = sb("key", [P, 2])
        keycmp = sb("keycmp", [P, 2, STEPS])
        m_k = sb("m_k", [P, STEPS])
        d_k = sb("d_k", [P, STEPS])
        tab_f = sb("tab_f", [1, 3, STEPS])
        dst_i = sb("dst_i", [P, EC], I32)
        dst_f = sb("dst_f", [P, EC])
        padrow = sb("padrow", [1, EPAD + 8 - E_IN])
        padsrc = sb("padsrc", [1, EPAD - E_IN], U32)
        W = sb("W", [P, 2, C + 2 * H])
        attb = sb("attb", [P, 2, C])
        wprod = sb("wprod", [P, 2, 2, C])
        fWs = sb("fWs", [P, 2, C])
        fWr = sb("fWr", [P, 2, C])
        lnwb = sb("lnwb", [P, C])
        lnbb = sb("lnbb", [P, C])
        fbc = sb("fbc", [P, 2])
        rowmean = sb("rowmean", [P, 2])
        bcol = sb("bcol", [P, 2])
        bdiag = sb("bdiag", [P, 2, P])
        xn = sb("xn", [P, 2, C])
        xT = sb("xT", [P, 2, 2, P])
        hrow = sb("hrow", [P, 2, C + 2 * H])
        ps_xt = [pb(f"ps_xt{i}") for i in range(2)]
        ps_h = [pb(f"ps_h{i}") for i in range(2)]
        ps_wt = [pb(f"ps_wt{i}") for i in range(2)]
        ps_b = pb("ps_b")
        ps_mk = pb("ps_mk")

        s_in = sem("s_in")
        s_pads = sem("s_pads")
        s_iota = sem("s_iota")
        s_ones = sem("s_ones")
        s_dstf = sem("s_dstf")
        s_edges = sem("s_edges")
        s_keycmp = sem("s_keycmp")
        s_mk = sem("s_mk")
        s_tab = sem("s_tab")
        s_stats = sem("s_stats")
        s_rstd = sem("s_rstd")
        s_xn = sem("s_xn")
        s_xt = sem("s_xt")
        s_xtc = sem("s_xtc")
        s_h = sem("s_h")
        s_hrow = sem("s_hrow")
        s_hst = [sem(f"s_hst{i}") for i in range(2)]
        s_wf = sem("s_wf")
        s_wt = sem("s_wt")
        s_dprep = sem("s_dprep")
        s_pprep = sem("s_pprep")
        TURN = 2

        with nc.Block() as block:
            @block.sync
            def _(sp):
                sp.wait_ge(s_pads, 1)
                sp.dma_start(X[:, 0:NT - 1, :], x[0:(NT - 1) * P, :].rearrange("(t p) c -> p t c", p=P)).then_inc(s_in, 16)
                sp.dma_start(X[0:TAIL, NT - 1, :], x[(NT - 1) * P:N, :]).then_inc(s_in, 16)
                sp.dma_start(dst_i[0:EL, :], dst.rearrange("(p c) -> p c", c=EC)).then_inc(s_in, 16)
                sp.dma_start(srcp[0:E_IN].rearrange("(p c) -> p c", c=EC),
                             src.rearrange("(p c) -> p c", c=EC)).then_inc(s_edges, 16)
                sp.dma_start(srcp[E_IN:EPAD].rearrange("(a n) -> a n", a=1), padsrc[:, :]).then_inc(s_edges, 16)
                sp.dma_start(dstp[0:1].rearrange("(a n) -> a n", a=1), padrow[:, 0:1]).then_inc(s_edges, 16)
                sp.dma_start(dstp[E_IN + 1:EPAD + 8].rearrange("(a n) -> a n", a=1), padrow[:, 1:]).then_inc(s_edges, 16)
                sp.wait_ge(s_dstf, 1)
                sp.dma_start(dstp[1:E_IN + 1].rearrange("(p c) -> p c", c=EC), dst_f[0:EL, :]).then_inc(s_edges, 16)

                def store_rows(i):
                    for u in range(TURN):
                        sp.wait_ge(s_hrow, i * TURN + (u + 1))
                        sp.nop(nofuse=True)
                        sp.dma_start(haug[bass.ds((i * TURN + u) * P, P), :], hrow[:, u, 0:ROW]).then_inc(s_hst[u], 16)
                        sp.dma_start(anode[bass.ds((i * TURN + u) * P, P), :], hrow[:, u, ROW:ROW + H]).then_inc(s_hst[u], 16)

                turns(sp, NX // TURN, store_rows)
                for u in range(TURN):
                    sp.wait_ge(s_hst[u], 32 * (NX // TURN))
                sp.wait_ge(s_edges, 16 * 5)

            @block.scalar
            def _(act):
                act.dma_start(W[:, :, 0:C], gW.rearrange("(k p) n -> p k n", p=P)).then_inc(s_in, 16)
                act.dma_start(fWs[:, :, :], fW.rearrange("(k p) n -> p k n", p=P)).then_inc(s_in, 16)
                act.dma_start(attb[:, 0, :], att_src.rearrange("h f -> (h f)").partition_broadcast(P)).then_inc(s_in, 16)
                act.dma_start(attb[:, 1, :], att_dst.rearrange("h f -> (h f)").partition_broadcast(P)).then_inc(s_in, 16)
                act.dma_start(lnwb[:, :], ln_w.partition_broadcast(P)).then_inc(s_in, 16)
                act.dma_start(lnbb[:, :], ln_b.partition_broadcast(P)).then_inc(s_in, 16)
                act.dma_start(gbb[:, :], gbias.partition_broadcast(P)).then_inc(s_in, 16)
                with nc.allow_non_contiguous_dma(reason="single elements: a bias as a column, block ends"):
                    act.dma_start(fbc[:, :], fb.rearrange("(k p) -> p k", p=P)).then_inc(s_in, 16)
                    ends = dst[0:(NB - 1) * BE].rearrange("(m e) -> m e", e=BE)
                    act.dma_start(key_i[:, 0:1], ends[0:P, BE - 1:BE]).then_inc(s_in, 16)
                    act.dma_start(key_i[0:MB, 1:2], ends[P:NB - 1, BE - 1:BE]).then_inc(s_in, 16)
                act.wait_ge(s_rstd, 1)

                def normalise(i):
                    for u in range(TURN):
                        wait_count(act, s_xt, i * TURN + (u + 1) - TURN)
                        act.nop(nofuse=True)
                        nc.scalar.activation(xn[:, u, :], X[:, bass.ds(i * TURN + u, 1), :], ACT.Identity,
                                             scale=rstd[:, bass.ds(i * TURN + u, 1)],
                                             bias=nmr[:, bass.ds(i * TURN + u, 1)]).then_inc(s_xn, 1)

                turns(act, NX // TURN, normalise)

            @block.gpsimd
            def _(pool):
                ch = Chain(pool, s_pprep)
                nc.gpsimd.memset(X[:, NT - 1:NX, :], 0.0)
                nc.gpsimd.memset(padsrc[:, :], 0)
                ch.add(nc.gpsimd.memset(padrow[:, :], 8191.0))
                ch.wait()
                nc.gpsimd.memset(padrow[:, 0:1], -1.0).then_inc(s_pads, 1)
                nc.gpsimd.iota(iota_i[:, :], pattern=[[1, STEPS]], base=0, channel_multiplier=0)
                nc.gpsimd.iota(part_i[:, :], pattern=[[0, 1]], base=0, channel_multiplier=1)
                nc.gpsimd.iota(lane_i[:, :], pattern=[[1, T]], base=0, channel_multiplier=T).then_inc(s_iota, 1)
                nc.gpsimd.memset(ones[:, :], 1.0).then_inc(s_ones, 1)
                ch.add(nc.gpsimd.memset(half_neg[:, :], -0.5))
                ch.wait()
                pool.wait_ge(s_stats, 1)
                ch.add(nc.gpsimd.tensor_tensor(rstd[:, :], ve[:, :], half_neg[:, :], ALU.pow))
                ch.wait()
                ch.add(nc.gpsimd.tensor_tensor(nmr[:, :], rstd[:, :], mv[:, :, 0], ALU.mult))
                ch.wait()
                nc.gpsimd.tensor_scalar(nmr[:, :], nmr[:, :], -1.0, None, ALU.mult).then_inc(s_rstd, 1)

            @block.vector
            def _(dve):
                ch = Chain(dve, s_dprep)
                v = nc.vector
                dve.wait_ge(s_iota, 1)
                v.tensor_copy(iota_k[:, :], iota_i[:, :])
                v.memset(head_reset[:, :], 0.0)
                v.memset(key[:, :], 1.0e9)
                ch.add(v.tensor_copy(part[:, :], part_i[:, :]))
                ch.wait()
                v.memset(head_reset[:, 0:1], NEG)
                v.tensor_scalar(ident[:, :], iota_k[:, 0:P], part[:, :], None, ALU.is_equal)
                v.tensor_scalar(is_last_lane[:, :], lane_i[:, :], float(BE - 1), None, ALU.is_equal)
                dve.wait_ge(s_in, 16 * 13)
                v.tensor_copy(dst_f[0:EL, :], dst_i[0:EL, :]).then_inc(s_dstf, 1)
                for t in range(NX):
                    last = v.bn_stats(bst[:, t, :], X[:, t, :])
                ch.add(last)
                ch.wait()
                for t in range(NX):
                    last = v.bn_aggr(mv[:, t, :], bst[:, t, :])
                ch.add(last)
                ch.wait()
                v.tensor_scalar(ve[:, :], mv[:, :, 1], EPS, None, ALU.add).then_inc(s_stats, 1)
                v.tensor_scalar(key_t[:, 0:1], key_i[:, 0:1], 7, None, ALU.arith_shift_right)
                ch.add(v.tensor_scalar(key_t[0:MB, 1:2], key_i[0:MB, 1:2], 7, None, ALU.arith_shift_right))
                ch.wait()
                v.tensor_tensor(key[:, 0:1], key_t[:, 0:1], part[:, :], ALU.add)
                ch.add(v.scalar_tensor_tensor(out=key[0:MB, 1:2], in0=key_t[0:MB, 1:2], scalar=float(P),
                                              in1=part[0:MB, :], op0=ALU.add, op1=ALU.add))
                ch.wait()
                v.tensor_scalar(keycmp[:, 0, :], iota_k[:, :], key[:, 0:1], None, ALU.is_gt)
                v.tensor_scalar(keycmp[:, 1, :], iota_k[:, :], key[:, 1:2], None, ALU.is_gt).then_inc(s_keycmp, 1)
                for k in range(2):
                    for a in range(2):
                        last = v.tensor_tensor(wprod[:, k, a, :], W[:, k, 0:C], attb[:, a, :], ALU.mult)
                ch.add(last)
                ch.wait()
                for k in range(2):
                    for a in range(2):
                        last = v.tensor_reduce(W[:, k, C + a * H:C + (a + 1) * H],
                                               wprod[:, k, a, :].rearrange("p (h f) -> p h f", h=H),
                                               axis=AX.X, op=ALU.add)
                last.then_inc(s_wf, 1)
                dve.wait_ge(s_wf, 1)
                for k in range(2):
                    v.tensor_tensor(fWr[:, k, :], fWs[:, k, :], lnwb[:, :], ALU.mult)
                    last = v.tensor_tensor(wprod[:, k, 0, :], fWs[:, k, :], lnbb[:, :], ALU.mult)
                ch.add(last)
                ch.wait()
                v.tensor_reduce(rowmean[:, :], fWr[:, :, :], axis=AX.X, op=ALU.add)
                ch.add(v.tensor_reduce(bcol[:, :], wprod[:, :, 0, :], axis=AX.X, op=ALU.add))
                ch.wait()
                v.tensor_scalar(rowmean[:, :], rowmean[:, :], 1.0 / C, None, ALU.mult)
                ch.add(v.tensor_tensor(bcol[:, :], bcol[:, :], fbc[:, :], ALU.add))
                ch.wait()
                for k in range(2):
                    v.tensor_scalar(fWr[:, k, :], fWr[:, k, :], rowmean[:, k:k + 1], None, ALU.subtract)
                    last = v.tensor_scalar(bdiag[:, k, :], ident[:, :], bcol[:, k:k + 1], HS, ALU.mult, ALU.mult)
                last.then_inc(s_wf, 1)
                dve.wait_ge(s_mk, 1)
                ch.add(v.tensor_copy(m_k[:, :], ps_mk[:, 0:STEPS]))
                ch.wait()
                ch.add(v.tensor_tensor(d_k[:, :], iota_k[:, :], m_k[:, :], ALU.subtract))
                ch.wait()
                v.tensor_scalar(base_k[:, :], d_k[:, :], float(P), None, ALU.mult)
                v.memset(first_k[:, 0:1], 1.0)
                ch.add(v.tensor_tensor(first_k[:, 1:], d_k[:, 1:], d_k[:, 0:STEPS - 1], ALU.subtract))
                ch.wait()
                v.tensor_scalar(keep_k[:, :], first_k[:, :], -1.0, 1.0, ALU.mult, ALU.add)
                v.tensor_scalar(tab_f[:, 0, :], m_k[0:1, :], float(BE), None, ALU.mult)
                v.tensor_scalar(tab_f[:, 1, :], base_k[0:1, :], 0.0, float((NT - 1) * P), ALU.max, ALU.min)
                ch.add(v.scalar_tensor_tensor(out=tab_f[:, 2, :], in0=base_k[0:1, :], scalar=-float(ZROW),
                                              in1=first_k[0:1, :], op0=ALU.add, op1=ALU.mult))
                ch.wait()
                ch.add(v.tensor_scalar(tab_f[:, 2, :], tab_f[:, 2, :], float(ZROW), 0.0, ALU.add, ALU.max))
                ch.wait()
                ch.add(v.tensor_scalar(tab_f[:, 2, :], tab_f[:, 2, :], float(ZROW), None, ALU.min))
                ch.wait()
                v.tensor_copy(tab_i[:, :, :], tab_f[:, :, :]).then_inc(s_tab, 1)
                dve.wait_ge(s_wt, 1)
                for a in range(2):
                    v.tensor_copy(WT[:, a, :], ps_wt[a][:, 0:C])
                v.tensor_copy(b100[:, :], ps_b[:, 0:C])

                def copy_rows(i):
                    for u in range(TURN):
                        dve.wait_ge(s_xt, i * TURN + (u + 1))
                        v.tensor_copy(xT[:, u, :, :], ps_xt[u][:, 0:C].rearrange("p (k n) -> p k n", k=2)).then_inc(s_xtc, 1)
                    for u in range(TURN):
                        dve.wait_ge(s_h, i * TURN + (u + 1))
                        wait_count(dve, s_hst[u], i * 32)
                        v.tensor_copy(hrow[:, u, :], ps_h[u][:, 0:C + 2 * H]).then_inc(s_hrow, 1)

                turns(dve, NX // TURN, copy_rows)

            @block.tensor
            def _(pe):
                mm = nc.tensor.matmul
                pe.wait_ge(s_ones, 1)
                pe.wait_ge(s_keycmp, 1)
                mm(ps_mk[:, 0:STEPS], ones[:, :], keycmp[:, 0, :], start=True, stop=False)
                mm(ps_mk[:, 0:STEPS], ones[:, :], keycmp[:, 1, :], start=False, stop=True).then_inc(s_mk, 1)
                pe.wait_ge(s_wf, 2)
                for a in range(2):
                    for k in range(2):
                        nc.tensor.transpose(ps_wt[a][:, k * P:(k + 1) * P], fWr[:, k, a * P:(a + 1) * P], ident[:, :])
                for k in range(2):
                    last = mm(ps_b[:, k * P:(k + 1) * P], ones[:, :], bdiag[:, k, :], start=True, stop=True)
                last.then_inc(s_wt, 1)

                def project(i):
                    for u in range(TURN):
                        pe.wait_ge(s_xn, i * TURN + (u + 1))
                        for k in range(2):
                            last = nc.tensor.transpose(ps_xt[u][:, k * P:(k + 1) * P], xn[:, u, k * P:(k + 1) * P], ident[:, :])
                        last.then_inc(s_xt, 1)
                    for u in range(TURN):
                        pe.wait_ge(s_xtc, i * TURN + (u + 1))
                        wait_count(pe, s_hrow, i * TURN + (u + 1) - TURN)
                        for k in range(2):
                            last = mm(ps_h[u][:, 0:C + 2 * H], xT[:, u, k, :], W[:, k, :], start=(k == 0), stop=(k == 1))
                        last.then_inc(s_h, 1)

                turns(pe, NX // TURN, project)


def attend(nc, sem, res, srcp, dstp, haug, anode, agg):
    ident, iota_k, is_last_lane, head_reset = (res[n] for n in ("ident", "iota_k", "is_last_lane", "head_reset"))
    base_k, first_k, keep_k, tab_i = (res[n] for n in ("base_k", "first_k", "keep_k", "tab_i"))
    BF16 = mybir.dt.bfloat16
    with ExitStack() as ctx:
        sb = lambda name, shape, dt=F32: ctx.enter_context(nc.sbuf_tensor(name, shape, dt))
        pb = lambda name, w=512, dt=F32: ctx.enter_context(nc.psum_tensor(name, [P, w], dt))
        idx = sb("idx", [P, R, T], U32)
        dw = sb("dw", [P, R, T + 2])
        selfr = sb("selfr", [P, R, ROW])
        an = sb("an", [P, R, H])
        G = sb("G", [P, R, T, ROW])
        acc = sb("acc", [P, R, ROW])
        neq = sb("neq", [P, R, T + 1])
        ff = sb("ff", [P, R, T])
        tr = sb("tr", [P, R, 2 * H])
        rel = sb("rel", [P, R, T])
        fadd = sb("fadd", [P, R, H * T])
        onehot_b = sb("onehot_b", [P, R, T, P], BF16)
        onehot = sb("onehot", [P, R, T, P])
        onehotT = sb("onehotT", [P, R, T, P])
        ident_b = sb("ident_b", [P, P], BF16)
        sv = sb("sv", [P, R, H * T])
        seg = sb("seg", [P, R, H * T])
        ffT = sb("ffT", [H, P])
        run = sb("run", [H, P + 1])
        ent = sb("ent", [P, R, H, T])
        full = sb("full", [P, R, H, T])
        lastmax = sb("lastmax", [P, R, T, H + 1])
        absent = sb("absent", [P, R])
        mx = sb("mx", [P, R, 2, H])
        zz = sb("zz", [P, R, 2, H])
        nodev = sb("nodev", [P, R, 3, H])
        dal = sb("dal", [P, R, H])
        alpha = sb("alpha", [P, R, H])
        scaled = sb("scaled", [P, R, ROW])
        ez = sb("ez", [P, R, T, H])
        lz = sb("lz", [P, R, T, H])
        el = sb("el", [P, R, T, H])
        TH = T // 2
        ps_ot = [pb(f"ps_ot{i}", TH * P, BF16) for i in range(2)]
        ps_tr = pb("ps_tr")
        ps_in = pb("ps_in")
        ps_mn = pb("ps_mn")
        ps_ex = pb("ps_ex")
        SB = 2
        ps_sum = [pb(f"ps_sum{i}") for i in range(SB)]
        SD = [(u - max(v for v in range(u - R, u) if (v % R) % SB == u % SB)) for u in range(R)]

        LOADS = 5
        s_ld = [sem(f"s_ld{u}") for u in range(R)]
        s_g = [sem(f"s_g{u}") for u in range(R)]
        s_st = [sem(f"s_st{u}") for u in range(R)]
        s_identb = sem("s_identb")
        s_onehot = sem("s_onehot")
        s_onehotf = sem("s_onehotf")
        s_ot = sem("s_ot")
        s_otc = sem("s_otc")
        s_tr = sem("s_tr")
        s_trT = sem("s_trT")
        s_ffT = sem("s_ffT")
        s_run = sem("s_run")
        s_enter = sem("s_enter")
        s_lastmax = sem("s_lastmax")
        s_mn = sem("s_mn")
        s_nodev = sem("s_nodev")
        s_ex = sem("s_ex")
        s_dal = sem("s_dal")
        s_alpha = sem("s_alpha")
        s_el = sem("s_el")
        s_w = sem("s_w")
        s_msg = sem("s_msg")
        s_sum = sem("s_sum")
        s_acc = sem("s_acc")
        s_datt = sem("s_datt")
        TURNS = STEPS // R

        def back(i, u, lag):
            if u >= lag:
                return i, u - lag
            return (i - 1, u - lag + R) if not (isinstance(i, int) and i == 0) else None

        def schedule(stages):
            def body(i):
                for u in range(R):
                    for stage, lag in stages:
                        at = back(i, u, lag)
                        if at:
                            stage(*at)
            return body

        def drain(stages, first=0):
            for extra in range(max(lag for _, lag in stages)):
                for stage, lag in stages:
                    if lag > extra:
                        k = STEPS + extra - lag
                        stage(k // R, k % R)

        with nc.Block() as block:
            @block.sync
            def _(sp):
                def load(i, u):
                    k = i * R + u
                    wait_count(sp, s_acc, k + 1 - R)
                    sp.nop(nofuse=True)
                    eb = sp.value_load(tab_i[0:1, 0, bass.ds(k, 1)], min_val=0, max_val=EPAD - BE)
                    nb = sp.value_load(tab_i[0:1, 1, bass.ds(k, 1)], min_val=0, max_val=(NT - 1) * P)
                    zb = sp.value_load(tab_i[0:1, 2, bass.ds(k, 1)], min_val=0, max_val=ZROW)
                    sp.dma_start(idx[:, u, :], srcp[bass.ds(eb, BE)].rearrange("(p t) -> p t", t=T)).then_inc(s_ld[u], 16)
                    sp.dma_start(dw[:, u, 0:T], dstp[bass.ds(eb, BE)].rearrange("(p t) -> p t", t=T)).then_inc(s_ld[u], 16)
                    sp.dma_start(dw[:, u, T:T + 2],
                                 dstp[bass.ds(eb + T, BE)].rearrange("(p t) -> p t", t=T)[:, 0:2]).then_inc(s_ld[u], 16)
                    sp.dma_start(selfr[:, u, :], haug[bass.ds(zb, P), :]).then_inc(s_ld[u], 16)
                    sp.dma_start(an[:, u, :], anode[bass.ds(nb, P), :]).then_inc(s_ld[u], 16)

                def store(i, u):
                    k = i * R + u
                    sp.wait_ge(s_acc, k + 1)
                    sp.nop(nofuse=True)
                    if u:
                        sp.wait_ge(s_st[u - 1], (i + 1) * 16)
                    else:
                        wait_count(sp, s_st[R - 1], i * 16)
                    sp.nop(nofuse=True)
                    nb = sp.value_load(tab_i[0:1, 1, bass.ds(k, 1)], min_val=0, max_val=(NT - 1) * P)
                    sp.dma_start(agg[bass.ds(nb, P), :], acc[:, u, :]).then_inc(s_st[u], 16)

                stages = [(load, 0), (store, LAG)]
                turns(sp, TURNS, schedule(stages), written=2)
                drain(stages)
                for u in range(R):
                    sp.wait_ge(s_st[u], TURNS * 16)

            @block.gpsimd
            def _(pool):
                def gather(i, u):
                    pool.wait_ge(s_ld[u], (i + 1) * (16 * LOADS))
                    pool.nop(nofuse=True)
                    for t in range(T):
                        pool.indirect_dma_start(
                            out=G[:, u, t, :], out_offset=None, in_=haug[:, :],
                            in_offset=bass.IndirectOffsetOnAxis(ap=idx[:, u, t:t + 1], axis=0),
                        ).then_inc(s_g[u], 16)

                turns(pool, TURNS, schedule([(gather, 0)]))

            @block.scalar
            def _(act):
                def flags(i, u):
                    act.wait_ge(s_trT, i * R + (u + 1))
                    nc.scalar.activation(ffT[:, :], ps_tr[0:H, P:2 * P], ACT.Copy).then_inc(s_ffT, 1)

                def onehots(i, u):
                    k = i * R + u
                    act.wait_ge(s_onehot, k + 1)
                    nc.scalar.activation(onehot[:, u, :, :], onehot_b[:, u, :, :], ACT.Copy).then_inc(s_onehotf, 1)
                    act.wait_ge(s_ot, k + 1)
                    for b in range(2):
                        last = nc.scalar.activation(onehotT[:, u, b * TH:(b + 1) * TH, :],
                                                    ps_ot[b][:, :].rearrange("p (t e) -> p t e", e=P), ACT.Copy)
                    last.then_inc(s_otc, 1)

                def rescale(i, u):
                    act.wait_ge(s_dal, i * R + (u + 1))
                    nc.scalar.activation(alpha[:, u, :], dal[:, u, :], ACT.Exp).then_inc(s_alpha, 1)

                def weights(i, u):
                    act.wait_ge(s_el, i * R + (u + 1))
                    nc.scalar.activation(G[:, u, :, C:ROW], el[:, u, :, :], ACT.Exp).then_inc(s_w, 1)

                stages = [(flags, 1), (onehots, 0), (rescale, 2), (weights, 2)]
                turns(act, TURNS, schedule(stages), written=2)
                drain(stages)

            @block.vector
            def _(dve):
                ch = Chain(dve, s_datt)
                v = nc.vector
                v.memset(run[:, :], NEG)
                v.memset(mx[:, R - 1, :, :], 0.0)
                v.tensor_copy(ident_b[:, :], ident[:, :]).then_inc(s_identb, 1)
                ch.add(v.memset(acc[:, R - 1, :], 0.0))
                ch.wait()

                def one_hots(i, u):
                    k = i * R + u
                    dve.wait_ge(s_ld[u], (i + 1) * (16 * LOADS))
                    ch.add(v.tensor_scalar(rel[:, u, :], dw[:, u, 1:T + 1], base_k[:, bass.ds(k, 1)], None, ALU.subtract))
                    v.tensor_tensor(neq[:, u, :], dw[:, u, 1:T + 2], dw[:, u, 0:T + 1], ALU.not_equal)
                    ch.add(v.tensor_scalar(ff[:, u, :], dw[:, u, 1:T + 1], dw[:, u, 0:1], NEG, ALU.not_equal, ALU.mult))
                    v.tensor_scalar(tr[:, u, H:2 * H], dw[:, u, T:T + 1].to_broadcast([P, H]), dw[:, u, 0:1], NEG,
                                    ALU.not_equal, ALU.mult)
                    ch.wait()
                    v.tensor_tensor(onehot_b[:, u, :, :], rel[:, u, :].unsqueeze(2).to_broadcast([P, T, P]),
                                    iota_k[:, 0:P].unsqueeze(1).to_broadcast([P, T, P]),
                                    ALU.is_equal).then_inc(s_onehot, 1)
                    v.scalar_tensor_tensor(out=fadd[:, u, :].rearrange("p (h t) -> p h t", h=H),
                                           in0=neq[:, u, 0:T].unsqueeze(1).to_broadcast([P, H, T]),
                                           scalar=NEG, in1=head_reset[:, :].unsqueeze(1).to_broadcast([P, H, T]),
                                           op0=ALU.mult, op1=ALU.add)
                    ch.add(v.tensor_tensor(lastmax[:, u, :, H], neq[:, u, 1:T + 1], is_last_lane[:, :], ALU.max))

                def segment_max(i, u):
                    dve.wait_ge(s_g[u], (i + 1) * (16 * T))
                    ch.add(v.tensor_copy(sv[:, u, :].rearrange("p (h t) -> p h t", h=H),
                                         G[:, u, :, C:ROW].rearrange("p t h -> p h t")))
                    ch.wait()
                    ch.add(v.tensor_tensor_scan(seg[:, u, :], fadd[:, u, :], sv[:, u, :], NEG, ALU.add, ALU.max))
                    ch.wait()
                    v.tensor_copy(tr[:, u, 0:H], seg[:, u, :].rearrange("p (h t) -> p h t", h=H)[:, :, T - 1]).then_inc(s_tr, 1)

                def over_partitions(i, u):
                    dve.wait_ge(s_ffT, i * R + (u + 1))
                    v.tensor_tensor_scan(run[:, 1:P + 1], ffT[:, :], ps_tr[0:H, 0:P], NEG,
                                         ALU.add, ALU.max).then_inc(s_run, 1)

                def segment_ends(i, u):
                    dve.wait_ge(s_enter, i * R + (u + 1))
                    ch.add(v.tensor_tensor(ent[:, u, :, :], ff[:, u, :].unsqueeze(1).to_broadcast([P, H, T]),
                                           ps_in[:, 0:H].unsqueeze(2).to_broadcast([P, H, T]), ALU.add))
                    ch.wait()
                    ch.add(v.tensor_tensor(full[:, u, :, :], seg[:, u, :].rearrange("p (h t) -> p h t", h=H),
                                           ent[:, u, :, :], ALU.max))
                    ch.wait()
                    v.tensor_tensor(lastmax[:, u, :, 0:H], full[:, u, :, :].rearrange("p h t -> p t h"),
                                    lastmax[:, u, :, H].unsqueeze(2).to_broadcast([P, T, H]),
                                    ALU.mult).then_inc(s_lastmax, 1)

                def node_max(i, u):
                    k = i * R + u
                    prev = (u - 1) % R
                    dve.wait_ge(s_mn, k + 1)
                    ch.add(v.tensor_scalar(absent[:, u:u + 1], ps_mn[:, H:H + 1], -1.0, -NEG, ALU.add, ALU.mult))
                    ch.add(v.scalar_tensor_tensor(out=mx[:, u, 0, :], in0=mx[:, prev, 1, :], scalar=keep_k[:, bass.ds(k, 1)],
                                                  in1=selfr[:, u, C:ROW], op0=ALU.mult, op1=ALU.add))
                    v.tensor_copy(nodev[:, u, 2, :], an[:, u, :])
                    ch.wait()
                    ch.add(v.scalar_tensor_tensor(out=mx[:, u, 1, :], in0=ps_mn[:, 0:H], scalar=absent[:, u:u + 1],
                                                  in1=mx[:, u, 0, :], op0=ALU.add, op1=ALU.max))
                    ch.wait()
                    ch.add(v.tensor_tensor(zz[:, u, :, :], mx[:, u, :, :],
                                           an[:, u, :].unsqueeze(1).to_broadcast([P, 2, H]), ALU.add))
                    ch.wait()
                    v.scalar_tensor_tensor(out=nodev[:, u, 0:2, :], in0=zz[:, u, :, :], scalar=SLOPE, in1=zz[:, u, :, :],
                                           op0=ALU.mult, op1=ALU.max).then_inc(s_nodev, 1)
                    dve.wait_ge(s_nodev, k + 1)
                    v.tensor_tensor(dal[:, u, :], nodev[:, u, 0, :], nodev[:, u, 1, :], ALU.subtract).then_inc(s_dal, 1)

                def logits(i, u):
                    dve.wait_ge(s_ex, i * R + (u + 1))
                    exv = ps_ex[:, 0:T * 2 * H].rearrange("p (t j h) -> p t j h", t=T, j=2)
                    ch.add(v.tensor_tensor(ez[:, u, :, :], G[:, u, :, C:ROW], exv[:, :, 1, :], ALU.add))
                    ch.wait()
                    ch.add(v.scalar_tensor_tensor(out=lz[:, u, :, :], in0=ez[:, u, :, :], scalar=SLOPE, in1=ez[:, u, :, :],
                                                  op0=ALU.mult, op1=ALU.max))
                    ch.wait()
                    ch.add(v.tensor_tensor(ez[:, u, :, :], lz[:, u, :, :], exv[:, :, 0, :], ALU.subtract))
                    ch.wait()
                    v.tensor_scalar(el[:, u, :, :], ez[:, u, :, :], 0.0, None, ALU.min).then_inc(s_el, 1)

                def messages(b):
                    def half(i, u):
                        dve.wait_ge(s_w, i * R + (u + 1))
                        gh = G[:, u, b * TH:(b + 1) * TH, 0:C].rearrange("p t (h f) -> p t h f", h=H)
                        v.tensor_tensor(gh, gh, G[:, u, b * TH:(b + 1) * TH, C:ROW].unsqueeze(3)
                                        .to_broadcast([P, TH, H, HID]), ALU.mult).then_inc(s_msg, 1)
                    return half

                def rescaled(i, u):
                    k = i * R + u
                    prev = (u - 1) % R
                    keep, first = keep_k[:, bass.ds(k, 1)], first_k[:, bass.ds(k, 1)]
                    wait_count(dve, s_acc, k)
                    v.scalar_tensor_tensor(out=scaled[:, u, 0:C], in0=acc[:, prev, 0:C], scalar=keep,
                                           in1=selfr[:, u, 0:C], op0=ALU.mult, op1=ALU.add)
                    ch.add(v.tensor_scalar(scaled[:, u, C:ROW], acc[:, prev, C:ROW], keep, first, ALU.mult, ALU.add))
                    dve.wait_ge(s_alpha, k + 1)
                    dve.nop(nofuse=True)
                    ch.wait()
                    v.tensor_tensor(scaled[:, u, 0:C].rearrange("p (h f) -> p h f", h=H),
                                    scaled[:, u, 0:C].rearrange("p (h f) -> p h f", h=H),
                                    alpha[:, u, :].unsqueeze(2).to_broadcast([P, H, HID]), ALU.mult)
                    ch.add(v.tensor_tensor(scaled[:, u, C:ROW], scaled[:, u, C:ROW], alpha[:, u, :], ALU.mult))

                def running_sums(i, u):
                    k = i * R + u
                    dve.wait_ge(s_sum, k + 1)
                    wait_count(dve, s_st[u], i * 16)
                    dve.nop(nofuse=True)
                    ch.wait()
                    v.tensor_tensor(acc[:, u, :], scaled[:, u, :], ps_sum[u % SB][:, 0:ROW], ALU.add).then_inc(s_acc, 1)

                stages = [(segment_max, 1), (segment_ends, 2), (running_sums, 4), (messages(0), 3),
                          (over_partitions, 1), (one_hots, 0), (node_max, 2), (messages(1), 3), (rescaled, 3), (logits, 2)]
                turns(dve, TURNS, schedule(stages), ch, written=2)
                drain(stages)

            @block.tensor
            def _(pe):
                mm, xp = nc.tensor.matmul, nc.tensor.transpose

                def transposed_onehots(i, u):
                    k = i * R + u
                    pe.wait_ge(s_onehot, k + 1)
                    wait_count(pe, s_otc, k)
                    for t in range(T):
                        last = xp(ps_ot[t // TH][:, (t % TH) * P:(t % TH + 1) * P], onehot_b[:, u, t, :], ident_b[:, :])
                    last.then_inc(s_ot, 1)

                def last_values(i, u):
                    k = i * R + u
                    pe.wait_ge(s_tr, k + 1)
                    wait_count(pe, s_run, k)
                    xp(ps_tr[0:H, 0:P], tr[:, u, 0:H], ident[:, :])
                    xp(ps_tr[0:H, P:2 * P], tr[:, u, H:2 * H], ident[:, :]).then_inc(s_trT, 1)

                def entering(i, u):
                    k = i * R + u
                    pe.wait_ge(s_run, k + 1)
                    wait_count(pe, s_lastmax, k)
                    mm(ps_in[:, 0:H], run[:, 0:P], ident[0:H, 0:H], start=True, stop=True).then_inc(s_enter, 1)

                def block_max(i, u):
                    k = i * R + u
                    pe.wait_ge(s_onehotf, k + 1)
                    pe.wait_ge(s_lastmax, k + 1)
                    wait_count(pe, s_nodev, k)
                    for t in range(T):
                        last = mm(ps_mn[:, 0:H + 1], onehot[:, u, t, :], lastmax[:, u, t, :], start=(t == 0), stop=(t == T - 1))
                    last.then_inc(s_mn, 1)

                def at_edges(i, u):
                    k = i * R + u
                    pe.wait_ge(s_otc, k + 1)
                    pe.wait_ge(s_nodev, k + 1)
                    wait_count(pe, s_el, k)
                    for t in range(T):
                        last = mm(ps_ex[:, t * 2 * H:(t + 1) * 2 * H], onehotT[:, u, t, :],
                                  nodev[:, u, 1:3, :].rearrange("p j h -> p (j h)"), start=True, stop=True)
                    last.then_inc(s_ex, 1)

                def sums(b):
                    def half(i, u):
                        k = i * R + u
                        if b == 0:
                            wait_count(pe, s_acc, k + 1 - SD[u])
                        pe.wait_ge(s_msg, 2 * k + (b + 1))
                        for t in range(b * TH, (b + 1) * TH):
                            last = mm(ps_sum[u % SB][:, 0:ROW], onehot[:, u, t, :], G[:, u, t, :],
                                      start=(t == 0), stop=(t == T - 1))
                        if b:
                            last.then_inc(s_sum, 1)
                    return half

                pe.wait_ge(s_identb, 1)
                stages = [(last_values, 1), (block_max, 2), (sums(0), 3), (entering, 1), (transposed_onehots, 0),
                          (at_edges, 2), (sums(1), 3)]
                turns(pe, TURNS, schedule(stages), written=2)
                drain(stages)


def scan_ffn(nc, sem, res, agg, out):
    X, ident, mv, rstd, nmr, ve, bst, half_neg = (res[n] for n in ("X", "ident", "mv", "rstd", "nmr", "ve", "bst", "half_neg"))
    WT, b100, gbb = res["WT"], res["b100"], res["gbb"]
    QT = 7
    assert NT % QT == 0
    with ExitStack() as ctx:
        sb = lambda name, shape, dt=F32: ctx.enter_context(nc.sbuf_tensor(name, shape, dt))
        pb = lambda name: ctx.enter_context(nc.psum_tensor(name, [P, 512], F32))
        Hs = sb("Hs", [P, NX, C])
        den = sb("den", [P, NT, H])
        rden = sb("rden", [P, NT, H])
        th = sb("th", [P, U, CH * C])
        h1 = sb("h1", [P, U, CH * C])
        h2 = sb("h2", [P, U, CH * C])
        h2T = sb("h2T", [P, U, CH * C])
        cst = sb("cst", [P, U, CH, 6])
        cmv = sb("cmv", [P, U, CH, 2])
        cve = sb("cve", [P, U, CH])
        r100 = sb("r100", [P, U, CH])
        ps_x = [pb(f"ps_x{i}") for i in range(3)]
        ps_g = [pb(f"ps_g{i}") for i in range(U)]
        XB = [0, 1, 2, 0, 1]
        XD = [2, 2, 5, 3, 3]
        s_agg = sem("s_aggin")
        s_den = sem("s_den")
        s_x1var = sem("s_x1var")
        s_x1root = sem("s_x1root")
        s_aff = sem("s_aff")
        s_tanh = sem("s_tanh")
        s_add = sem("s_add")
        s_silu = sem("s_silu")
        s_ve = sem("s_ve")
        s_r = sem("s_r")
        s_xp = sem("s_xp")
        s_h2T = sem("s_h2T")
        s_prod = sem("s_prod")
        s_dffn = sem("s_dffn")
        s_bn = sem("s_bn")
        s_pffn = sem("s_pffn")
        s_fin = sem("s_fin")
        s_out = sem("s_out")
        TURNS = NC // U
        ALL = ITERS * NC

        def chunk_rows(ap, j):
            return ap[:, bass.ds(j * CH, CH), :].rearrange("p a c -> p (a c)")

        def iterate(eng, turn):
            turn(0, 0)
            turn(U, U)
            with eng.Fori(2, TURNS) as b:
                turn(b * U, b * U)
            with eng.Fori(1, ITERS) as it:
                with eng.Fori(0, TURNS) as b:
                    turn(it * NC + b * U, b * U)

        with nc.Block() as block:
            @block.sync
            def _(sp):
                for b in range(NT // QT):
                    rows = agg[b * QT * P:(b + 1) * QT * P, :]
                    sp.dma_start(Hs[:, b * QT:(b + 1) * QT, :], rows[:, 0:C].rearrange("(t p) c -> p t c", p=P)).then_inc(s_agg, 16)
                sp.dma_start(den[:, :, :], agg[:, C:ROW].rearrange("(t p) h -> p t h", p=P)).then_inc(s_den, 16)
                sp.wait_ge(s_fin, 1)
                sp.dma_start(out[0:(NT - 1) * P, :].rearrange("(t p) c -> p t c", p=P), X[:, 0:NT - 1, :]).then_inc(s_out, 16)
                sp.dma_start(out[(NT - 1) * P:N, :], X[0:TAIL, NT - 1, :]).then_inc(s_out, 16)
                sp.wait_ge(s_out, 32)

            @block.gpsimd
            def _(pool):
                ch = Chain(pool, s_pffn)
                pool.wait_ge(s_x1var, 1)
                ch.add(nc.gpsimd.tensor_tensor(rstd[:, :], ve[:, :], half_neg[:, :], ALU.pow))
                ch.wait()
                nc.gpsimd.tensor_tensor(nmr[:, :], rstd[:, :], mv[:, :, 0], ALU.mult).then_inc(s_x1root, 1)

                def turn(q0, j0):
                    for u in range(U):
                        q = q0 + u
                        pool.wait_ge(s_tanh, q + 1)
                        wait_count(pool, s_silu, q + 1 - U)
                        pool.nop(nofuse=True)
                        nc.gpsimd.tensor_tensor(h1[:, u, :], chunk_rows(Hs, j0 + u), th[:, u, :], ALU.add).then_inc(s_add, 1)
                        if not (isinstance(q, int) and q < 3):
                            root(q - 3, (u - 3) % U)

                def root(q, u):
                    pool.wait_ge(s_ve, q + 1)
                    pool.wait_ge(s_aff, q + (NC + 1 - U))
                    nc.gpsimd.tensor_tensor(r100[:, u, :], cve[:, u, :], half_neg[:, 0:CH], ALU.pow).then_inc(s_r, 1)

                iterate(pool, turn)
                for q in range(ALL - 3, ALL):
                    root(q, q % U)

            @block.scalar
            def _(act):
                def silu(q, u):
                    act.wait_ge(s_add, q + 1)
                    wait_count(act, s_xp, q + 1 - U)
                    wait_count(act, s_ve, q + 1 - U)
                    nc.scalar.activation(h2[:, u, :], h1[:, u, :], ACT.Silu, scale=1.0 / HS).then_inc(s_silu, 1)

                def copy_t(q, u):
                    act.wait_ge(s_xp, q + 1)
                    wait_count(act, s_prod, q + 1 - U)
                    nc.scalar.activation(h2T[:, u, :], ps_x[XB[u]][:, :], ACT.Copy).then_inc(s_h2T, 1)

                def turn(q0, j0):
                    for u in range(U):
                        q = q0 + u
                        act.wait_ge(s_aff, q + 1)
                        wait_count(act, s_add, q + 1 - U)
                        act.nop(nofuse=True)
                        nc.scalar.activation(th[:, u, :], chunk_rows(Hs, j0 + u), ACT.Tanh, scale=1.0 / HS).then_inc(s_tanh, 1)
                        if not (isinstance(q, int) and q < 1):
                            silu(q - 1, (u - 1) % U)
                        if not (isinstance(q, int) and q < 3):
                            copy_t(q - 3, (u - 3) % U)

                iterate(act, turn)
                silu(ALL - 1, (ALL - 1) % U)
                for q in range(ALL - 3, ALL):
                    copy_t(q, q % U)

            @block.vector
            def _(dve):
                ch = Chain(dve, s_dffn)
                v = nc.vector
                v.memset(Hs[:, NT:NX, :], 0.0)
                dve.wait_ge(s_den, 16)
                ch.add(v.reciprocal(rden[:, :, :], den[:, :, :]))
                ch.wait()
                dve.wait_ge(s_agg, 16 * (NT // QT))
                for b in range(NT // QT):
                    hs = Hs[:, b * QT:(b + 1) * QT, :].rearrange("p t (h f) -> p (t h) f", h=H)
                    rd = rden[:, b * QT:(b + 1) * QT, :].rearrange("p t h -> p (t h)").unsqueeze(2)
                    ch.add(v.tensor_tensor(hs, hs, rd.to_broadcast([P, QT * H, HID]), ALU.mult))
                ch.wait()
                for b in range(NT // QT):
                    hs = Hs[:, b * QT:(b + 1) * QT, :]
                    ch.add(v.tensor_tensor(hs, hs, gbb[:, :].unsqueeze(1).to_broadcast([P, QT, C]), ALU.add))
                ch.wait()
                for b in range(NT // QT):
                    xs = X[:, b * QT:(b + 1) * QT, :].rearrange("p t c -> p (t c)")
                    hs = Hs[:, b * QT:(b + 1) * QT, :].rearrange("p t c -> p (t c)")
                    ch.add(v.scalar_tensor_tensor(out=xs, in0=hs, scalar=0.0, in1=xs, op0=ALU.max, op1=ALU.add))
                ch.wait()
                for t in range(NX):
                    last = v.bn_stats(bst[:, t, :], X[:, t, :])
                ch.add(last)
                ch.wait()
                for t in range(NX):
                    last = v.bn_aggr(mv[:, t, :], bst[:, t, :])
                ch.add(last)
                ch.wait()
                v.tensor_scalar(ve[:, :], mv[:, :, 1], EPS, None, ALU.add).then_inc(s_x1var, 1)
                dve.wait_ge(s_x1root, 1)
                v.tensor_scalar(nmr[:, :], nmr[:, :], -HS, None, ALU.mult)
                ch.add(v.tensor_scalar(rstd[:, :], rstd[:, :], HS, None, ALU.mult))
                ch.wait()
                for j in range(NC):
                    for a in range(CH):
                        t = j * CH + a
                        last = v.tensor_scalar(Hs[:, t, :], X[:, t, :], rstd[:, t:t + 1], nmr[:, t:t + 1], ALU.mult, ALU.add)
                    last.then_inc(s_aff, 1)

                def stats(q, u):
                    dve.wait_ge(s_silu, q + 1)
                    for a in range(CH):
                        last = v.bn_stats(cst[:, u, a, :], h2[:, u, a * C:(a + 1) * C])
                    last.then_inc(s_bn, 1)
                    dve.wait_ge(s_bn, 2 * q + 1)
                    dve.nop(nofuse=True)
                    for a in range(CH):
                        last = v.bn_aggr(cmv[:, u, a, :], cst[:, u, a, :])
                    last.then_inc(s_bn, 1)
                    dve.wait_ge(s_bn, 2 * q + 2)
                    wait_count(dve, s_r, q + 1 - U)
                    v.tensor_scalar(cve[:, u, :], cmv[:, u, :, 1], EPS, 1.0 / (HS * HS), ALU.add, ALU.mult).then_inc(s_ve, 1)

                def affine(q, j, u):
                    dve.wait_ge(s_prod, q + 1)
                    dve.wait_ge(s_r, q + 1)
                    for a in range(CH):
                        last = v.scalar_tensor_tensor(out=Hs[:, bass.ds(j * CH + a, 1), :].rearrange("p a c -> p (a c)"),
                                                      in0=ps_g[u][:, a * C:(a + 1) * C],
                                                      scalar=r100[:, u, a:a + 1], in1=b100[:, :], op0=ALU.mult, op1=ALU.add)
                    last.then_inc(s_aff, 1)

                LEAD = 3
                for q in range(LEAD):
                    stats(q, q)

                def turn(q0, j0, lead=U):
                    for u in range(U):
                        if u < lead:
                            stats(q0 + (u + LEAD), (u + LEAD) % U)
                        affine(q0 + u, j0 + u, u)

                turn(0, 0)
                with dve.Fori(1, TURNS) as b:
                    turn(b * U, b * U)
                with dve.Fori(1, ITERS - 1) as it:
                    with dve.Fori(0, TURNS) as b:
                        turn(it * NC + b * U, b * U)
                with dve.Fori(0, TURNS - 1) as b:
                    turn(b * U + (ITERS - 1) * NC, b * U)
                turn(ALL - U, NC - U, lead=U - LEAD)
                dve.wait_ge(s_aff, NC + ALL)
                for b in range(NT // QT):
                    xs = X[:, b * QT:(b + 1) * QT, :].rearrange("p t c -> p (t c)")
                    hs = Hs[:, b * QT:(b + 1) * QT, :].rearrange("p t c -> p (t c)")
                    last = v.scalar_tensor_tensor(out=xs, in0=hs, scalar=1.0 / HS, in1=xs, op0=ALU.mult, op1=ALU.add)
                last.then_inc(s_fin, 1)

            @block.tensor
            def _(pe):
                def transposes(q, u):
                    pe.wait_ge(s_silu, q + 1)
                    wait_count(pe, s_h2T, q + 1 - XD[u])
                    for n in range(CH * 2):
                        last = nc.tensor.transpose(ps_x[XB[u]][:, n * P:(n + 1) * P], h2[:, u, n * P:(n + 1) * P], ident[:, :])
                    last.then_inc(s_xp, 1)

                def product(q, u):
                    pe.wait_ge(s_h2T, q + 1)
                    pe.wait_ge(s_aff, q + (NC + 1 - U))
                    for a in range(CH):
                        for k in range(2):
                            last = nc.tensor.matmul(ps_g[u][:, a * C:(a + 1) * C], h2T[:, u, (a * 2 + k) * P:(a * 2 + k + 1) * P],
                                                    WT[:, k, :], start=(k == 0), stop=(k == 1))
                    last.then_inc(s_prod, 1)

                def turn(q0, j0):
                    for u in range(U):
                        q = q0 + u
                        transposes(q, u)
                        if not (isinstance(q, int) and q < 2):
                            product(q - 2, (u - 2) % U)

                iterate(pe, turn)
                for q in range(ALL - 2, ALL):
                    product(q, q % U)


def kernel(x, src, dst, L0_gnn_W, L0_gnn_att_src, L0_gnn_att_dst, L0_gnn_bias,
           L0_ffn_ln_w, L0_ffn_ln_b, L0_ffn_W, L0_ffn_b):
    import numpy as np
    import concourse.bacc as bacc
    from concourse.bass_utils import run_bass_kernel_spmd

    arrays = {
        "x": x, "src": src, "dst": dst, "gnn_W": L0_gnn_W, "att_src": L0_gnn_att_src,
        "att_dst": L0_gnn_att_dst, "gnn_bias": L0_gnn_bias, "ln_w": L0_ffn_ln_w, "ln_b": L0_ffn_ln_b,
        "ffn_W": L0_ffn_W, "ffn_b": L0_ffn_b,
    }
    arrays = {n: np.ascontiguousarray(a) for n, a in arrays.items()}
    arrays["src"] = arrays["src"].view(np.uint32)
    nc = bacc.Bacc("TRN2", target_bir_lowering=False, num_devices=1)
    args = [nc.dram_tensor(n, a.shape, mybir.dt.from_np(a.dtype), kind="ExternalInput").ap() for n, a in arrays.items()]
    out = nc.dram_tensor("out", (N, C), F32, kind="ExternalOutput").ap()
    build(nc, *args, out)
    return run_bass_kernel_spmd(nc, [arrays], core_ids=[0]).results[0]["out"]
```

```python
import concourse.bass as bass
from concourse import mybir
from contextlib import ExitStack

F32 = mybir.dt.float32
I32 = mybir.dt.int32
U32 = mybir.dt.uint32
ALU = mybir.AluOpType
ACT = mybir.ActivationFunctionType
AX = mybir.AxisListType

N, C, H, HID = 6250, 256, 4, 64
E_IN = 206250
P = 128
NT = -(-N // P)
NX = NT + NT % 2
TAIL = N - (NT - 1) * P
NODES = NX * P
ZROW = NT * P
HR = HID + 1
ROW = H * HR

T = 8
BE = P * T
NB = -(-E_IN // BE)
EPAD = NB * BE
STEPS = NB - 1 + NT
R = 5
RG = 4
GB = -(-NB // RG) * RG
assert STEPS % R == 0
LAG = R + 1

QT = 7
assert NT % QT == 0
EL = 125
assert E_IN % EL == 0
EC = E_IN // EL

NEG = -1.0e30
SLOPE = 0.2
EPS = 1e-5

ITERS = 30
CH = 2
NC = NX // CH
U = 5
assert NC % U == 0 and CH == 2
HS = 100.0


class Chain:

    def __init__(self, eng, sem, done=0):
        self.eng, self.sem, self.base, self.n, self.reg = eng, sem, done, 0, 0

    def add(self, ins):
        self.n += 1
        return ins.then_inc(self.sem, 1)

    def wait(self):
        self.eng.wait_ge(self.sem, self.reg + (self.base + self.n))


def turns(eng, count, body, chain=None, written=1):
    for i in range(written):
        start = chain.n if chain else 0
        body(i)
    if chain:
        per = chain.n - start
        chain.base, chain.n = chain.base + chain.n, 0
    with eng.Fori(written, count) as i:
        if chain:
            chain.reg = (i - written) * per
        body(i)
    if chain:
        assert chain.n == per
        chain.base, chain.n, chain.reg = chain.base + per * (count - written), 0, 0


def back(i, u, lag, ring):
    turns_back = (max(lag - u, 0) + ring - 1) // ring
    if isinstance(i, int) and i < turns_back:
        return None
    return i - turns_back, u - lag + turns_back * ring


def schedule(stages, ring):
    def body(i):
        for u in range(ring):
            for stage, lag in stages:
                at = back(i, u, lag, ring)
                if at:
                    stage(*at)
    return body


def drain(stages, ring, steps):
    for extra in range(max(lag for _, lag in stages)):
        for stage, lag in stages:
            if lag > extra:
                k = steps + extra - lag
                stage(k // ring, k % ring)


def part_tiles(b):
    return b * QT, NX if b == NT // QT - 1 else (b + 1) * QT


def load_part(eng, x, X, b, sem):
    full = min((b + 1) * QT, NT - 1)
    eng.dma_start(X[:, b * QT:full, :], x[b * QT * P:full * P, :].rearrange("(t p) c -> p t c", p=P)).then_inc(sem, 16)
    if full < (b + 1) * QT:
        eng.dma_start(X[0:TAIL, full, :], x[full * P:N, :]).then_inc(sem, 16)


def wait_count(eng, sem, count):
    if isinstance(count, int) and count <= 0:
        return
    eng.wait_ge(sem, count)


def build(nc, x, src, dst, gW, att_src, att_dst, gbias, ln_w, ln_b, fW, fb, out):
    srcp = nc.dram_tensor("srcp", (GB * BE,), U32).ap()
    dstp = nc.dram_tensor("dstp", (EPAD + 8,), F32).ap()
    haug = nc.dram_tensor("haug", (NODES, ROW), F32).ap()
    anode = nc.dram_tensor("anode", (NODES, H), F32).ap()
    agg = nc.dram_tensor("agg", (NT * P, ROW), F32).ap()

    with ExitStack() as ctx:
        sb = lambda name, shape, dt=F32: ctx.enter_context(nc.sbuf_tensor(name, shape, dt))
        sem = lambda name: ctx.enter_context(nc.semaphore(name))
        res = dict(
            ident=sb("ident", [P, P]),
            iota_k=sb("iota_k", [P, STEPS]),
            is_last_lane=sb("is_last_lane", [P, T]),
            head_reset=sb("head_reset", [P, T]),
            half_neg=sb("half_neg", [P, NX]),
            bst=sb("bst", [P, NX, 6]),
            mv=sb("mv", [P, NX, 2]),
            ve=sb("ve", [P, NX]),
            rstd=sb("rstd", [P, NX]),
            nmr=sb("nmr", [P, NX]),
            base_k=sb("base_k", [P, STEPS]),
            first_k=sb("first_k", [P, STEPS]),
            keep_k=sb("keep_k", [P, STEPS]),
            tab_i=sb("tab_i", [1, 4, STEPS], I32),
            free_i=sb("free_i", [1, NB - 1], I32),
            idx_all=sb("idx_all", [P, GB, T], U32),
            WT=sb("WT", [P, 2, C]),
            b100=sb("b100", [P, C]),
            gbb=sb("gbb", [P, C]),
        )
        prepare(nc, sem, res, x, src, dst, gW, att_src, att_dst, gbias, ln_w, ln_b, fW, fb,
                srcp, dstp, haug, anode)
        attend(nc, sem, res, srcp, dstp, haug, anode, agg)
        scan_ffn(nc, sem, res, x, agg, out)


def prepare(nc, sem, res, x, src, dst, gW, att_src, att_dst, gbias, ln_w, ln_b, fW, fb,
            srcp, dstp, haug, anode):
    ident, iota_k, mv, rstd, nmr, ve = (res[n] for n in ("ident", "iota_k", "mv", "rstd", "nmr", "ve"))
    bst, half_neg, is_last_lane, head_reset = (res[n] for n in ("bst", "half_neg", "is_last_lane", "head_reset"))
    base_k, first_k, keep_k, tab_i = (res[n] for n in ("base_k", "first_k", "keep_k", "tab_i"))
    WT, b100, gbb = res["WT"], res["b100"], res["gbb"]
    free_i, idx_all = res["free_i"], res["idx_all"]
    MB = NB - 1 - P
    TURN = 10
    RS = 5
    assert NX % TURN == 0 and TURN % RS == 0
    with ExitStack() as ctx:
        sb = lambda name, shape, dt=F32: ctx.enter_context(nc.sbuf_tensor(name, shape, dt))
        pb = lambda name: ctx.enter_context(nc.psum_tensor(name, [P, 512], F32))
        X = sb("X", [P, NX, C])
        ones = sb("ones", [P, P])
        iota_i = sb("iota_i", [P, STEPS], I32)
        part_i = sb("part_i", [P, 1], I32)
        part = sb("part", [P, 1])
        lane_i = sb("lane_i", [P, T], I32)
        end_i = sb("end_i", [1, NB - 1], I32)
        end_t = sb("end_t", [1, NB - 1], I32)
        end_f = sb("end_f", [1, NB - 1])
        zero_f = sb("zero_f", [1, NB - 1])
        end_m = sb("end_m", [1, NB - 1])
        keyrow = sb("keyrow", [1, NB - 1])
        key = sb("key", [P, 2])
        keycmp = sb("keycmp", [P, 2, STEPS])
        m_k = sb("m_k", [P, STEPS])
        d_k = sb("d_k", [P, STEPS])
        tab_f = sb("tab_f", [1, 4, STEPS])
        dst_i = sb("dst_i", [P, EC], I32)
        dst_f = sb("dst_f", [P, EC])
        padrow = sb("padrow", [1, EPAD + 8 - E_IN])
        padsrc = sb("padsrc", [1, GB * BE - E_IN], U32)
        W = sb("W", [P, 2, C])
        W2 = sb("W2", [P, 2, ROW + H])
        attb = sb("attb", [P, 2, C])
        wprod = sb("wprod", [P, 2, 2, C])
        fWs = sb("fWs", [P, 2, C])
        fWr = sb("fWr", [P, 2, C])
        lnwb = sb("lnwb", [P, C])
        lnbb = sb("lnbb", [P, C])
        fbc = sb("fbc", [P, 2])
        rowmean = sb("rowmean", [P, 2])
        bcol = sb("bcol", [P, 2])
        bdiag = sb("bdiag", [P, 2, P])
        xn = sb("xn", [P, 2, C])
        xT = sb("xT", [P, 2, 2, P])
        hrow = sb("hrow", [P, RS, ROW + H])
        ps_xt = [pb(f"ps_xt{i}") for i in range(2)]
        ps_h = [pb(f"ps_h{i}") for i in range(2)]
        ps_wt = [pb(f"ps_wt{i}") for i in range(2)]
        ps_b = pb("ps_b")
        ps_mk = pb("ps_mk")

        s_in = sem("s_in")
        s_dst = sem("s_dst")
        s_end = sem("s_end")
        s_x = [sem(f"s_x{b}") for b in range(NT // QT)]
        s_pads = sem("s_pads")
        s_iota = sem("s_iota")
        s_ones = sem("s_ones")
        s_dstf = sem("s_dstf")
        s_edges = sem("s_edges")
        s_keyrow = sem("s_keyrow")
        s_keycol = sem("s_keycol")
        s_keycmp = sem("s_keycmp")
        s_idx = sem("s_idx")
        s_mk = sem("s_mk")
        s_tab = sem("s_tab")
        s_stats = sem("s_stats")
        s_rstd = sem("s_rstd")
        s_xn = sem("s_xn")
        s_xt = sem("s_xt")
        s_xtc = sem("s_xtc")
        s_h = sem("s_h")
        s_hrow = sem("s_hrow")
        s_hst = [sem(f"s_hst{i}") for i in range(RS)]
        s_wf = sem("s_wf")
        s_wt = sem("s_wt")
        s_dprep = sem("s_dprep")
        s_pprep = sem("s_pprep")
        with nc.Block() as block:
            @block.sync
            def _(sp):
                sp.dma_start(dst_i[0:EL, :], dst.rearrange("(p c) -> p c", c=EC)).then_inc(s_dst, 16)
                sp.wait_ge(s_pads, 1)
                for b in range(NT // QT):
                    load_part(sp, x, X, b, s_x[b])
                sp.dma_start(srcp[0:E_IN].rearrange("(p c) -> p c", c=EC),
                             src.rearrange("(p c) -> p c", c=EC)).then_inc(s_edges, 16)
                sp.dma_start(srcp[E_IN:GB * BE].rearrange("(a n) -> a n", a=1), padsrc[:, :]).then_inc(s_edges, 16)
                sp.dma_start(dstp[0:1].rearrange("(a n) -> a n", a=1), padrow[:, 0:1]).then_inc(s_edges, 16)
                sp.dma_start(dstp[E_IN + 1:EPAD + 8].rearrange("(a n) -> a n", a=1), padrow[:, 1:]).then_inc(s_edges, 16)
                sp.wait_ge(s_dstf, 1)
                sp.dma_start(dstp[1:E_IN + 1].rearrange("(p c) -> p c", c=EC), dst_f[0:EL, :]).then_inc(s_edges, 16)
                sp.wait_ge(s_edges, 16 * 5)
                sp.dma_start(idx_all[:, :, :], srcp.rearrange("(b p t) -> p b t", p=P, t=T)).then_inc(s_idx, 16)

                def store_rows(i):
                    for u in range(TURN):
                        sp.wait_ge(s_hrow, i * TURN + (u + 1))
                        sp.nop(nofuse=True)
                        sp.dma_start(haug[bass.ds((i * TURN + u) * P, P), :], hrow[:, u % RS, 0:ROW]).then_inc(s_hst[u % RS], 16)
                        sp.dma_start(anode[bass.ds((i * TURN + u) * P, P), :], hrow[:, u % RS, ROW:ROW + H]).then_inc(s_hst[u % RS], 16)

                turns(sp, NX // TURN, store_rows)
                for u in range(RS):
                    sp.wait_ge(s_hst[u], 32 * (NX // RS))
                sp.wait_ge(s_idx, 16)

            @block.scalar
            def _(act):
                act.dma_start(W[:, :, :], gW.rearrange("(k p) n -> p k n", p=P)).then_inc(s_in, 16)
                act.dma_start(fWs[:, :, :], fW.rearrange("(k p) n -> p k n", p=P)).then_inc(s_in, 16)
                act.dma_start(attb[:, 0, :], att_src.rearrange("h f -> (h f)").partition_broadcast(P)).then_inc(s_in, 16)
                act.dma_start(attb[:, 1, :], att_dst.rearrange("h f -> (h f)").partition_broadcast(P)).then_inc(s_in, 16)
                act.dma_start(lnwb[:, :], ln_w.partition_broadcast(P)).then_inc(s_in, 16)
                act.dma_start(lnbb[:, :], ln_b.partition_broadcast(P)).then_inc(s_in, 16)
                act.dma_start(gbb[:, :], gbias.partition_broadcast(P)).then_inc(s_in, 16)
                with nc.allow_non_contiguous_dma(reason="single elements: a bias as a column, block ends"):
                    act.dma_start(fbc[:, :], fb.rearrange("(k p) -> p k", p=P)).then_inc(s_in, 16)
                    ends = dst[0:(NB - 1) * BE].rearrange("(m e) -> e m", e=BE)
                    act.dma_start(end_i[:, :], ends[BE - 1:BE, :]).then_inc(s_end, 16)

                def normalise(i):
                    for u in range(TURN):
                        wait_count(act, s_xt, i * TURN + (u + 1) - 2)
                        act.wait_ge(s_rstd, i * TURN + (u + 1))
                        act.nop(nofuse=True)
                        nc.scalar.activation(xn[:, u % 2, :], X[:, bass.ds(i * TURN + u, 1), :], ACT.Identity,
                                             scale=rstd[:, bass.ds(i * TURN + u, 1)],
                                             bias=nmr[:, bass.ds(i * TURN + u, 1)]).then_inc(s_xn, 1)

                turns(act, NX // TURN, normalise)

            @block.gpsimd
            def _(pool):
                ch = Chain(pool, s_pprep)
                nc.gpsimd.memset(X[:, NT - 1:NX, :], 0.0)
                nc.gpsimd.memset(padsrc[:, :], 0)
                ch.add(nc.gpsimd.memset(padrow[:, :], 8191.0))
                ch.wait()
                nc.gpsimd.memset(padrow[:, 0:1], -1.0).then_inc(s_pads, 1)
                nc.gpsimd.iota(iota_i[:, :], pattern=[[1, STEPS]], base=0, channel_multiplier=0)
                nc.gpsimd.iota(part_i[:, :], pattern=[[0, 1]], base=0, channel_multiplier=1)
                nc.gpsimd.iota(lane_i[:, :], pattern=[[1, T]], base=0, channel_multiplier=T).then_inc(s_iota, 1)
                nc.gpsimd.memset(ones[:, :], 1.0).then_inc(s_ones, 1)
                ch.add(nc.gpsimd.memset(half_neg[:, :], -0.5))
                ch.wait()
                for b in range(NT // QT):
                    t0, t1 = part_tiles(b)
                    pool.wait_ge(s_stats, b + 1)
                    ch.add(nc.gpsimd.tensor_tensor(rstd[:, t0:t1], ve[:, t0:t1], half_neg[:, t0:t1], ALU.pow))
                    ch.wait()
                    ch.add(nc.gpsimd.tensor_tensor(nmr[:, t0:t1], rstd[:, t0:t1], mv[:, t0:t1, 0], ALU.mult))
                    ch.wait()
                    nc.gpsimd.tensor_scalar(nmr[:, t0:t1], nmr[:, t0:t1], -1.0, None, ALU.mult).then_inc(s_rstd, t1 - t0)

            @block.vector
            def _(dve):
                ch = Chain(dve, s_dprep)
                v = nc.vector
                dve.wait_ge(s_iota, 1)
                v.tensor_copy(iota_k[:, :], iota_i[:, :])
                v.memset(head_reset[:, :], 0.0)
                v.memset(key[:, :], 1.0e9)
                ch.add(v.tensor_copy(part[:, :], part_i[:, :]))
                ch.wait()
                v.memset(head_reset[:, 0:1], NEG)
                v.tensor_scalar(ident[:, :], iota_k[:, 0:P], part[:, :], None, ALU.is_equal)
                v.tensor_scalar(is_last_lane[:, :], lane_i[:, :], float(BE - 1), None, ALU.is_equal)
                dve.wait_ge(s_dst, 16)
                v.tensor_copy(dst_f[0:EL, :], dst_i[0:EL, :]).then_inc(s_dstf, 1)
                dve.wait_ge(s_end, 16)
                v.memset(zero_f[:, :], 0.0)
                ch.add(v.tensor_scalar(end_t[:, :], end_i[:, :], 7, None, ALU.arith_shift_right))
                ch.wait()
                ch.add(v.tensor_copy(end_f[:, :], end_t[:, :]))
                ch.wait()
                ch.add(v.tensor_tensor_scan(end_m[:, :], zero_f[:, :], end_f[:, :], 0.0, ALU.add, ALU.max))
                ch.wait()
                v.tensor_tensor(keyrow[:, :], end_m[:, :], iota_k[0:1, 0:NB - 1], ALU.add).then_inc(s_keyrow, 1)
                dve.wait_ge(s_keyrow, 1)
                ch.add(v.tensor_scalar(end_f[:, :], keyrow[:, :], 1.0, None, ALU.add))
                ch.wait()
                v.tensor_copy(free_i[:, :], end_f[:, :])
                dve.wait_ge(s_keycol, 1)
                v.tensor_copy(key[:, 0:1], ps_b[:, 0:1])
                ch.add(v.tensor_copy(key[0:MB, 1:2], ps_b[0:MB, 1:2]))
                ch.wait()
                v.tensor_scalar(keycmp[:, 0, :], iota_k[:, :], key[:, 0:1], None, ALU.is_gt)
                v.tensor_scalar(keycmp[:, 1, :], iota_k[:, :], key[:, 1:2], None, ALU.is_gt).then_inc(s_keycmp, 1)
                dve.wait_ge(s_in, 16 * 8)
                for k in range(2):
                    for a in range(2):
                        last = v.tensor_tensor(wprod[:, k, a, :], W[:, k, :], attb[:, a, :], ALU.mult)
                ch.add(last)
                ch.wait()
                for k in range(2):
                    for a in range(2):
                        at = W2[:, k, HID:ROW:HR] if a == 0 else W2[:, k, ROW:ROW + H]
                        last = v.tensor_reduce(at,
                                               wprod[:, k, a, :].rearrange("p (h f) -> p h f", h=H),
                                               axis=AX.X, op=ALU.add)
                for k in range(2):
                    last = v.tensor_copy(W2[:, k, 0:ROW].rearrange("p (h f) -> p h f", h=H)[:, :, 0:HID],
                                         W[:, k, :].rearrange("p (h f) -> p h f", h=H))
                last.then_inc(s_wf, 1)
                dve.wait_ge(s_wf, 1)
                for k in range(2):
                    v.tensor_tensor(fWr[:, k, :], fWs[:, k, :], lnwb[:, :], ALU.mult)
                    last = v.tensor_tensor(wprod[:, k, 0, :], fWs[:, k, :], lnbb[:, :], ALU.mult)
                ch.add(last)
                ch.wait()
                v.tensor_reduce(rowmean[:, :], fWr[:, :, :], axis=AX.X, op=ALU.add)
                ch.add(v.tensor_reduce(bcol[:, :], wprod[:, :, 0, :], axis=AX.X, op=ALU.add))
                ch.wait()
                v.tensor_scalar(rowmean[:, :], rowmean[:, :], 1.0 / C, None, ALU.mult)
                ch.add(v.tensor_tensor(bcol[:, :], bcol[:, :], fbc[:, :], ALU.add))
                ch.wait()
                for k in range(2):
                    v.tensor_scalar(fWr[:, k, :], fWr[:, k, :], rowmean[:, k:k + 1], None, ALU.subtract)
                    last = v.tensor_scalar(bdiag[:, k, :], ident[:, :], bcol[:, k:k + 1], HS, ALU.mult, ALU.mult)
                last.then_inc(s_wf, 1)
                dve.wait_ge(s_mk, 1)
                ch.add(v.tensor_copy(m_k[:, :], ps_mk[:, 0:STEPS]))
                ch.wait()
                ch.add(v.tensor_tensor(d_k[:, :], iota_k[:, :], m_k[:, :], ALU.subtract))
                ch.wait()
                v.tensor_scalar(base_k[:, :], d_k[:, :], float(P), None, ALU.mult)
                v.memset(first_k[:, 0:1], 1.0)
                ch.add(v.tensor_tensor(first_k[:, 1:], d_k[:, 1:], d_k[:, 0:STEPS - 1], ALU.subtract))
                ch.wait()
                v.tensor_scalar(keep_k[:, :], first_k[:, :], -1.0, 1.0, ALU.mult, ALU.add)
                v.tensor_scalar(tab_f[:, 0, :], m_k[0:1, :], float(BE), None, ALU.mult)
                v.tensor_scalar(tab_f[:, 3, :], m_k[0:1, :], 1.0, None, ALU.add)
                v.tensor_scalar(tab_f[:, 1, :], base_k[0:1, :], 0.0, float((NT - 1) * P), ALU.max, ALU.min)
                ch.add(v.scalar_tensor_tensor(out=tab_f[:, 2, :], in0=base_k[0:1, :], scalar=-float(ZROW),
                                              in1=first_k[0:1, :], op0=ALU.add, op1=ALU.mult))
                ch.wait()
                ch.add(v.tensor_scalar(tab_f[:, 2, :], tab_f[:, 2, :], float(ZROW), 0.0, ALU.add, ALU.max))
                ch.wait()
                ch.add(v.tensor_scalar(tab_f[:, 2, :], tab_f[:, 2, :], float(ZROW), None, ALU.min))
                ch.wait()
                v.tensor_copy(tab_i[:, :, :], tab_f[:, :, :]).then_inc(s_tab, 1)
                for b in range(NT // QT):
                    t0, t1 = part_tiles(b)
                    dve.wait_ge(s_x[b], 16 if b < NT // QT - 1 else 32)
                    for t in range(t0, t1):
                        last = v.bn_stats(bst[:, t, :], X[:, t, :])
                    ch.add(last)
                    ch.wait()
                    for t in range(t0, t1):
                        last = v.bn_aggr(mv[:, t, :], bst[:, t, :])
                    ch.add(last)
                    ch.wait()
                    v.tensor_scalar(ve[:, t0:t1], mv[:, t0:t1, 1], EPS, None, ALU.add).then_inc(s_stats, 1)
                dve.wait_ge(s_wt, 1)
                for a in range(2):
                    v.tensor_copy(WT[:, a, :], ps_wt[a][:, 0:C])
                v.tensor_copy(b100[:, :], ps_b[:, 0:C])

                def copy_x(i, u):
                    dve.wait_ge(s_xt, i * TURN + (u + 1))
                    v.tensor_copy(xT[:, u % 2, :, :], ps_xt[u % 2][:, 0:C].rearrange("p (k n) -> p k n", k=2)).then_inc(s_xtc, 1)

                def copy_h(i, u):
                    dve.wait_ge(s_h, i * TURN + (u + 1))
                    wait_count(dve, s_hst[u % RS], i * (32 * TURN // RS) + u // RS * 32)
                    v.tensor_copy(hrow[:, u % RS, :], ps_h[u % 2][:, 0:ROW + H]).then_inc(s_hrow, 1)

                stages = [(copy_h, 2), (copy_x, 0)]
                turns(dve, NX // TURN, schedule(stages, TURN), written=2)
                drain(stages, TURN, NX)

            @block.tensor
            def _(pe):
                mm = nc.tensor.matmul
                pe.wait_ge(s_ones, 1)
                pe.wait_ge(s_keyrow, 1)
                mm(ps_b[:, 0:1], keyrow[:, 0:P], ident[0:1, 0:1], start=True, stop=True)
                mm(ps_b[0:MB, 1:2], keyrow[:, P:NB - 1], ident[0:1, 0:1], start=True, stop=True).then_inc(s_keycol, 1)
                pe.wait_ge(s_keycmp, 1)
                mm(ps_mk[:, 0:STEPS], ones[:, :], keycmp[:, 0, :], start=True, stop=False)
                mm(ps_mk[:, 0:STEPS], ones[:, :], keycmp[:, 1, :], start=False, stop=True).then_inc(s_mk, 1)
                pe.wait_ge(s_wf, 2)
                for a in range(2):
                    for k in range(2):
                        nc.tensor.transpose(ps_wt[a][:, k * P:(k + 1) * P], fWr[:, k, a * P:(a + 1) * P], ident[:, :])
                for k in range(2):
                    last = mm(ps_b[:, k * P:(k + 1) * P], ones[:, :], bdiag[:, k, :], start=True, stop=True)
                last.then_inc(s_wt, 1)

                def transposes(i, u):
                    pe.wait_ge(s_xn, i * TURN + (u + 1))
                    for k in range(2):
                        last = nc.tensor.transpose(ps_xt[u % 2][:, k * P:(k + 1) * P], xn[:, u % 2, k * P:(k + 1) * P], ident[:, :])
                    last.then_inc(s_xt, 1)

                def project(i, u):
                    pe.wait_ge(s_xtc, i * TURN + (u + 1))
                    wait_count(pe, s_hrow, i * TURN + (u + 1) - 2)
                    for k in range(2):
                        last = mm(ps_h[u % 2][:, 0:ROW + H], xT[:, u % 2, k, :], W2[:, k, :], start=(k == 0), stop=(k == 1))
                    last.then_inc(s_h, 1)

                stages = [(transposes, 0), (project, 1)]
                turns(pe, NX // TURN, schedule(stages, TURN), written=2)
                drain(stages, TURN, NX)


def attend(nc, sem, res, srcp, dstp, haug, anode, agg):
    ident, iota_k, is_last_lane, head_reset = (res[n] for n in ("ident", "iota_k", "is_last_lane", "head_reset"))
    base_k, first_k, keep_k, tab_i = (res[n] for n in ("base_k", "first_k", "keep_k", "tab_i"))
    free_i, idx_all = res["free_i"], res["idx_all"]
    BF16 = mybir.dt.bfloat16
    with ExitStack() as ctx:
        sb = lambda name, shape, dt=F32: ctx.enter_context(nc.sbuf_tensor(name, shape, dt))
        pb = lambda name, w=512, dt=F32: ctx.enter_context(nc.psum_tensor(name, [P, w], dt))
        idx = sb("idx", [P, 2, T], U32)
        G = sb("G", [P, RG, T, ROW])
        M = sb("M", [P, R, T, ROW])
        dw = sb("dw", [P, R, T + 2])
        selfr = sb("selfr", [P, R, ROW])
        acc = sb("acc", [P, R, ROW])
        neq = sb("neq", [P, R, T + 1])
        ff = sb("ff", [P, R, T])
        rel = sb("rel", [P, R, T])
        fadd = sb("fadd", [P, R, H * T])
        onehot_b = sb("onehot_b", [P, R, T, P], BF16)
        onehot = sb("onehot", [P, R, T, P])
        onehotT = sb("onehotT", [P, R, T, P])
        ident_b = sb("ident_b", [P, P], BF16)
        sv = sb("sv", [P, R, H * T])
        seg = sb("seg", [P, R, H * T])
        ffT = sb("ffT", [H, P])
        run = sb("run", [H, P + 1])
        ent = sb("ent", [P, R, H, T])
        full = sb("full", [P, R, H, T])
        lastmax = sb("lastmax", [P, R, T, H + 1])
        absent = sb("absent", [P, R])
        mx = sb("mx", [P, R, 2, H])
        zz = sb("zz", [P, R, 2, H])
        nodev = sb("nodev", [P, R, 3, H])
        dal = sb("dal", [P, R, H])
        alpha = sb("alpha", [P, R, H])
        scaled = sb("scaled", [P, R, ROW])
        ez = sb("ez", [P, R, T, H])
        lz = sb("lz", [P, R, T, H])
        el = sb("el", [P, R, T, H])
        TH = T // 2
        ps_ot = pb("ps_ot", T * P, BF16)
        ps_tr = pb("ps_tr")
        ps_in = pb("ps_in")
        ps_mn = pb("ps_mn")
        ps_ex = pb("ps_ex")
        SB = 3
        ps_sum = [pb(f"ps_sum{i}") for i in range(SB)]
        SD = [(u - max(v for v in range(u - R, u) if (v % R) % SB == u % SB)) for u in range(R)]

        LOADS = 2
        s_ld = [sem(f"s_ld{u}") for u in range(R)]
        s_ldn = [sem(f"s_ldn{u}") for u in range(R)]
        s_g = [sem(f"s_g{u}") for u in range(RG)]
        s_idxc = sem("s_idxc")
        s_block = sem("s_block")
        s_st = [sem(f"s_st{u}") for u in range(R)]
        s_identb = sem("s_identb")
        s_onehot = sem("s_onehot")
        s_onehotf = sem("s_onehotf")
        s_ot = sem("s_ot")
        s_otc = sem("s_otc")
        s_taken = sem("s_taken")
        s_sv = sem("s_sv")
        s_seg = sem("s_seg")
        s_trT = sem("s_trT")
        s_ffT = sem("s_ffT")
        s_run = sem("s_run")
        s_enter = sem("s_enter")
        s_lastmax = sem("s_lastmax")
        s_mn = sem("s_mn")
        s_nodev = sem("s_nodev")
        s_ex = sem("s_ex")
        s_dal = sem("s_dal")
        s_carried = sem("s_carried")
        s_scaled = sem("s_scaled")
        s_alpha = sem("s_alpha")
        s_el = sem("s_el")
        s_relu = sem("s_relu")
        s_w = sem("s_w")
        s_msg = sem("s_msg")
        s_sum = sem("s_sum")
        s_acc = sem("s_acc")
        s_datt = sem("s_datt")
        TURNS = STEPS // R

        with nc.Block() as block:
            @block.sync
            def _(sp):
                def load_edges(i, u):
                    k = i * R + u
                    wait_count(sp, s_msg, 2 * (k + 1 - R))
                    sp.nop(nofuse=True)
                    eb = sp.value_load(tab_i[0:1, 0, bass.ds(k, 1)], min_val=0, max_val=EPAD - BE)
                    sp.dma_start(dw[:, u, 0:T], dstp[bass.ds(eb, BE)].rearrange("(p t) -> p t", t=T)).then_inc(s_ld[u], 16)
                    sp.dma_start(dw[:, u, T:T + 2],
                                 dstp[bass.ds(eb + T, BE)].rearrange("(p t) -> p t", t=T)[:, 0:2]).then_inc(s_ld[u], 16)

                def load_nodes(i, u):
                    k = i * R + u
                    wait_count(sp, s_acc, k + 1 - R)
                    sp.nop(nofuse=True)
                    nb = sp.value_load(tab_i[0:1, 1, bass.ds(k, 1)], min_val=0, max_val=(NT - 1) * P)
                    zb = sp.value_load(tab_i[0:1, 2, bass.ds(k, 1)], min_val=0, max_val=ZROW)
                    sp.dma_start(selfr[:, u, :], haug[bass.ds(zb, P), :]).then_inc(s_ldn[u], 16)
                    sp.dma_start(nodev[:, u, 0, :], anode[bass.ds(nb, P), :]).then_inc(s_ldn[u], 16)

                def store(i, u):
                    k = i * R + u
                    sp.wait_ge(s_acc, k + 1)
                    sp.nop(nofuse=True)
                    if u:
                        sp.wait_ge(s_st[u - 1], (i + 1) * 16)
                    else:
                        wait_count(sp, s_st[R - 1], i * 16)
                    sp.nop(nofuse=True)
                    nb = sp.value_load(tab_i[0:1, 1, bass.ds(k, 1)], min_val=0, max_val=(NT - 1) * P)
                    sp.dma_start(agg[bass.ds(nb, P), :], acc[:, u, :]).then_inc(s_st[u], 16)

                stages = [(load_edges, 0), (load_nodes, 1), (store, LAG)]
                turns(sp, TURNS, schedule(stages, R), written=2)
                drain(stages, R, STEPS)
                for u in range(R):
                    sp.wait_ge(s_st[u], TURNS * 16)

            @block.gpsimd
            def _(pool):
                def place(b, u):
                    nc.gpsimd.tensor_copy(idx[:, u % 2, :].unsqueeze(1), idx_all[:, bass.ds(b, 1), :]).then_inc(s_idxc, 1)

                def arrived(i, u):
                    pool.wait_ge(s_g[u], (i + 1) * (16 * T))
                    pool.nop(nofuse=True)
                    pool.sem_inc(s_block, 1)

                def gather(i):
                    later = not (isinstance(i, int) and i == 0)
                    for u in range(RG):
                        b = i * RG + u
                        if later:
                            done = pool.value_load(free_i[0:1, bass.ds(b - RG, 1)], min_val=1, max_val=STEPS)
                            pool.wait_ge(s_taken, done)
                            pool.nop(nofuse=True)
                        pool.wait_ge(s_idxc, b + 1)
                        pool.nop(nofuse=True)
                        for t in range(T):
                            pool.indirect_dma_start(
                                out=G[:, u, t, :], out_offset=None, in_=haug[:, :],
                                in_offset=bass.IndirectOffsetOnAxis(ap=idx[:, u % 2, t:t + 1], axis=0),
                            ).then_inc(s_g[u], 16)
                            if t == 2 and u:
                                arrived(i, u - 1)
                            elif t == 2 and later:
                                arrived(i - 1, RG - 1)
                            if t == 3 and not (isinstance(b, int) and b == GB - 1):
                                place(b + 1, u + 1)

                place(0, 0)
                gather(0)
                with pool.Fori(1, GB // RG - 1) as i:
                    gather(i)
                gather(GB // RG - 1)
                arrived(GB // RG - 1, RG - 1)

            @block.scalar
            def _(act):
                def flags(i, u):
                    act.wait_ge(s_trT, i * R + (u + 1))
                    nc.scalar.activation(ffT[:, :], ps_tr[0:H, P:2 * P], ACT.Copy).then_inc(s_ffT, 1)

                def take(i, u):
                    k = i * R + u
                    wait_count(act, s_acc, k + 1 - R)
                    act.nop(nofuse=True)
                    begun = act.value_load(tab_i[0:1, 3, bass.ds(k, 1)], min_val=1, max_val=NB)
                    slot = (begun - 1) % RG
                    act.wait_ge(s_block, begun)
                    act.nop(nofuse=True)
                    rows = G[:, bass.ds(slot, 1), :, :].rearrange("p a t c -> p (a t) c")
                    nc.scalar.activation(sv[:, u, :].rearrange("p (h t) -> p h t", h=H),
                                         rows[:, :, HID:ROW:HR].rearrange("p t h -> p h t"), ACT.Copy).then_inc(s_sv, 1)
                    nc.scalar.activation(M[:, u, :, :], rows, ACT.Copy).then_inc(s_taken, 1)

                def onehots(i, u):
                    k = i * R + u
                    act.wait_ge(s_onehot, k + 1)
                    nc.scalar.activation(onehot[:, u, :, :], onehot_b[:, u, :, :], ACT.Copy).then_inc(s_onehotf, 1)

                def transposed(i, u):
                    k = i * R + u
                    act.wait_ge(s_ot, k + 1)
                    nc.scalar.activation(onehotT[:, u, :, :], ps_ot[:, :].rearrange("p (t e) -> p t e", e=P),
                                         ACT.Copy).then_inc(s_otc, 1)

                def rescale(i, u):
                    act.wait_ge(s_dal, i * R + (u + 1))
                    nc.scalar.activation(alpha[:, u, :], dal[:, u, :], ACT.Exp).then_inc(s_alpha, 1)

                def weights(i, u):
                    act.wait_ge(s_el, i * R + (u + 1))
                    nc.scalar.activation(ez[:, u, :, :], el[:, u, :, :], ACT.Relu).then_inc(s_relu, 1)
                    act.wait_ge(s_relu, i * R + (u + 1))
                    nc.scalar.activation(M[:, u, :, HID:ROW:HR], ez[:, u, :, :], ACT.Exp, scale=-1.0).then_inc(s_w, 1)

                def rescaled(i, u):
                    act.wait_ge(s_carried, i * R + (u + 1))
                    act.wait_ge(s_alpha, i * R + (u + 1))
                    for h in range(H):
                        sh = scaled[:, u, h * HR:(h + 1) * HR]
                        last = nc.scalar.activation(sh, sh, ACT.Copy, scale=alpha[:, u, h:h + 1])
                    last.then_inc(s_scaled, 1)

                stages = [(flags, 1), (onehots, 0), (weights, 3), (rescaled, 4), (transposed, 0), (rescale, 2), (take, 0)]
                turns(act, TURNS, schedule(stages, R), written=2)
                drain(stages, R, STEPS)

            @block.vector
            def _(dve):
                ch = Chain(dve, s_datt)
                v = nc.vector
                v.memset(run[:, :], NEG)
                v.memset(mx[:, R - 1, :, :], 0.0)
                v.tensor_copy(ident_b[:, :], ident[:, :]).then_inc(s_identb, 1)
                ch.add(v.memset(acc[:, R - 1, :], 0.0))
                ch.wait()

                def one_hots(i, u):
                    k = i * R + u
                    dve.wait_ge(s_ld[u], (i + 1) * (16 * LOADS))
                    ch.add(v.tensor_scalar(rel[:, u, :], dw[:, u, 1:T + 1], base_k[:, bass.ds(k, 1)], None, ALU.subtract))
                    v.tensor_tensor(neq[:, u, :], dw[:, u, 1:T + 2], dw[:, u, 0:T + 1], ALU.not_equal)
                    ch.add(v.tensor_scalar(ff[:, u, :], dw[:, u, 1:T + 1], dw[:, u, 0:1], NEG, ALU.not_equal, ALU.mult))
                    ch.wait()
                    v.tensor_tensor(onehot_b[:, u, :, :], rel[:, u, :].unsqueeze(2).to_broadcast([P, T, P]),
                                    iota_k[:, 0:P].unsqueeze(1).to_broadcast([P, T, P]),
                                    ALU.is_equal).then_inc(s_onehot, 1)
                    ch.add(v.scalar_tensor_tensor(out=fadd[:, u, :].rearrange("p (h t) -> p h t", h=H),
                                           in0=neq[:, u, 0:T].unsqueeze(1).to_broadcast([P, H, T]),
                                           scalar=NEG, in1=head_reset[:, :].unsqueeze(1).to_broadcast([P, H, T]),
                                           op0=ALU.mult, op1=ALU.add))
                    ch.add(v.tensor_tensor(lastmax[:, u, :, H], neq[:, u, 1:T + 1], is_last_lane[:, :], ALU.max))

                def segment_max(i, u):
                    dve.wait_ge(s_sv, i * R + (u + 1))
                    ch.wait()
                    v.tensor_tensor_scan(seg[:, u, :], fadd[:, u, :], sv[:, u, :], NEG, ALU.add, ALU.max).then_inc(s_seg, 1)

                def over_partitions(i, u):
                    dve.wait_ge(s_ffT, i * R + (u + 1))
                    v.tensor_tensor_scan(run[:, 1:P + 1], ffT[:, :], ps_tr[0:H, 0:P], NEG,
                                         ALU.add, ALU.max).then_inc(s_run, 1)

                def entered(i, u):
                    dve.wait_ge(s_enter, i * R + (u + 1))
                    ch.add(v.tensor_tensor(ent[:, u, :, :], ff[:, u, :].unsqueeze(1).to_broadcast([P, H, T]),
                                           ps_in[:, 0:H].unsqueeze(2).to_broadcast([P, H, T]), ALU.add))

                def in_block(i, u):
                    ch.wait()
                    ch.add(v.tensor_tensor(full[:, u, :, :], seg[:, u, :].rearrange("p (h t) -> p h t", h=H),
                                           ent[:, u, :, :], ALU.max))

                def segment_ends(i, u):
                    ch.wait()
                    v.tensor_tensor(lastmax[:, u, :, 0:H], full[:, u, :, :].rearrange("p h t -> p t h"),
                                    lastmax[:, u, :, H].unsqueeze(2).to_broadcast([P, T, H]),
                                    ALU.mult).then_inc(s_lastmax, 1)

                def max_before(i, u):
                    k = i * R + u
                    prev = (u - 1) % R
                    dve.wait_ge(s_ldn[u], (i + 1) * (16 * LOADS))
                    dve.wait_ge(s_mn, k + 1)
                    ch.add(v.tensor_scalar(absent[:, u:u + 1], ps_mn[:, H:H + 1], -1.0, -NEG, ALU.add, ALU.mult))
                    ch.add(v.scalar_tensor_tensor(out=mx[:, u, 1, :], in0=mx[:, prev, 0, :], scalar=keep_k[:, bass.ds(k, 1)],
                                                  in1=selfr[:, u, HID:ROW:HR], op0=ALU.mult, op1=ALU.add))

                def logit_sum(i, u):
                    dve.wait_ge(s_ex, i * R + (u + 1))
                    ch.add(v.tensor_tensor(ez[:, u, :, :], sv[:, u, :].rearrange("p (h t) -> p t h", h=H),
                                           exv()[:, :, 0, :], ALU.add))

                def max_now(i, u):
                    ch.wait()
                    ch.add(v.scalar_tensor_tensor(out=mx[:, u, 0, :], in0=ps_mn[:, 0:H], scalar=absent[:, u:u + 1],
                                                  in1=mx[:, u, 1, :], op0=ALU.add, op1=ALU.max))
                    ch.add(v.tensor_copy(selfr[:, u, HID:ROW:HR], first_k[:, bass.ds(i * R + u, 1)].to_broadcast([P, H])))

                def logit_leaky(i, u):
                    ch.wait()
                    ch.add(v.scalar_tensor_tensor(out=lz[:, u, :, :], in0=ez[:, u, :, :], scalar=SLOPE, in1=ez[:, u, :, :],
                                                  op0=ALU.mult, op1=ALU.max))

                def max_sum(i, u):
                    ch.wait()
                    ch.add(v.tensor_tensor(zz[:, u, :, :], mx[:, u, :, :],
                                           nodev[:, u, 0, :].unsqueeze(1).to_broadcast([P, 2, H]), ALU.add))

                def below_max(i, u):
                    ch.wait()
                    v.tensor_tensor(el[:, u, :, :], exv()[:, :, 1, :], lz[:, u, :, :], ALU.subtract).then_inc(s_el, 1)

                def max_leaky(i, u):
                    ch.wait()
                    v.scalar_tensor_tensor(out=nodev[:, u, 1:3, :], in0=zz[:, u, :, :], scalar=SLOPE, in1=zz[:, u, :, :],
                                           op0=ALU.mult, op1=ALU.max).then_inc(s_nodev, 1)

                def max_step(i, u):
                    k = i * R + u
                    dve.wait_ge(s_nodev, k + 1)
                    v.tensor_tensor(dal[:, u, :], nodev[:, u, 2, :], nodev[:, u, 1, :], ALU.subtract).then_inc(s_dal, 1)

                def exv():
                    return ps_ex[:, 0:T * 2 * H].rearrange("p (t j h) -> p t j h", t=T, j=2)

                def messages(b):
                    def half(i, u):
                        dve.wait_ge(s_w, i * R + (u + 1))
                        mh = M[:, u, b * TH:(b + 1) * TH, :].rearrange("p t (h f) -> p (t h) f", h=H)
                        v.tensor_tensor(mh[:, :, 0:HID], mh[:, :, 0:HID],
                                        mh[:, :, HID:HR].to_broadcast([P, TH * H, HID]), ALU.mult).then_inc(s_msg, 1)
                    return half

                def carried(i, u):
                    k = i * R + u
                    prev = (u - 1) % R
                    wait_count(dve, s_acc, k)
                    v.scalar_tensor_tensor(out=scaled[:, u, :], in0=acc[:, prev, :], scalar=keep_k[:, bass.ds(k, 1)],
                                           in1=selfr[:, u, :], op0=ALU.mult, op1=ALU.add).then_inc(s_carried, 1)

                def running_sums(i, u):
                    k = i * R + u
                    dve.wait_ge(s_sum, k + 1)
                    wait_count(dve, s_st[u], i * 16)
                    dve.nop(nofuse=True)
                    dve.wait_ge(s_scaled, k + 1)
                    v.tensor_tensor(acc[:, u, :], scaled[:, u, :], ps_sum[u % SB][:, 0:ROW], ALU.add).then_inc(s_acc, 1)

                stages = [(segment_max, 1), (entered, 2), (in_block, 2), (segment_ends, 2),
                          (one_hots, 0), (running_sums, 5), (over_partitions, 1), (carried, 4),
                          (logit_sum, 3), (max_before, 2), (logit_leaky, 3), (max_now, 2), (below_max, 3), (max_sum, 2),
                          (max_leaky, 2), (max_step, 2), (messages(0), 3), (messages(1), 3)]
                turns(dve, TURNS, schedule(stages, R), ch, written=2)
                drain(stages, R, STEPS)

            @block.tensor
            def _(pe):
                mm, xp = nc.tensor.matmul, nc.tensor.transpose

                def transposed_onehots(i, u):
                    k = i * R + u
                    pe.wait_ge(s_onehot, k + 1)
                    wait_count(pe, s_otc, k)
                    for t in range(T):
                        last = xp(ps_ot[:, t * P:(t + 1) * P], onehot_b[:, u, t, :], ident_b[:, :])
                    last.then_inc(s_ot, 1)

                def last_values(i, u):
                    k = i * R + u
                    pe.wait_ge(s_seg, k + 1)
                    wait_count(pe, s_run, k)
                    xp(ps_tr[0:H, 0:P], seg[:, u, T - 1:H * T:T], ident[:, :])
                    xp(ps_tr[0:H, P:2 * P], ff[:, u, T - 1:T].to_broadcast([P, H]), ident[:, :]).then_inc(s_trT, 1)

                def entering(i, u):
                    k = i * R + u
                    pe.wait_ge(s_run, k + 1)
                    wait_count(pe, s_lastmax, k)
                    mm(ps_in[:, 0:H], run[:, 0:P], ident[0:H, 0:H], start=True, stop=True).then_inc(s_enter, 1)

                def block_max(i, u):
                    k = i * R + u
                    pe.wait_ge(s_onehotf, k + 1)
                    pe.wait_ge(s_lastmax, k + 1)
                    wait_count(pe, s_nodev, k)
                    for t in range(T):
                        last = mm(ps_mn[:, 0:H + 1], onehot[:, u, t, :], lastmax[:, u, t, :], start=(t == 0), stop=(t == T - 1))
                    last.then_inc(s_mn, 1)

                def at_edges(i, u):
                    k = i * R + u
                    pe.wait_ge(s_otc, k + 1)
                    pe.wait_ge(s_nodev, k + 1)
                    wait_count(pe, s_el, k)
                    for t in range(T):
                        last = mm(ps_ex[:, t * 2 * H:(t + 1) * 2 * H], onehotT[:, u, t, :],
                                  nodev[:, u, 0:2, :].rearrange("p j h -> p (j h)"), start=True, stop=True)
                    last.then_inc(s_ex, 1)

                def sums(b):
                    def half(i, u):
                        k = i * R + u
                        if b == 0:
                            wait_count(pe, s_acc, k + 1 - SD[u])
                        pe.wait_ge(s_msg, 2 * k + (b + 1))
                        for t in range(b * TH, (b + 1) * TH):
                            last = mm(ps_sum[u % SB][:, 0:ROW], onehot[:, u, t, :], M[:, u, t, :],
                                      start=(t == 0), stop=(t == T - 1))
                        if b:
                            last.then_inc(s_sum, 1)
                    return half

                pe.wait_ge(s_identb, 1)
                stages = [(last_values, 1), (block_max, 2), (sums(0), 4), (entering, 1), (transposed_onehots, 0),
                          (at_edges, 2), (sums(1), 4)]
                turns(pe, TURNS, schedule(stages, R), written=2)
                drain(stages, R, STEPS)


def scan_ffn(nc, sem, res, x, agg, out):
    ident, mv, rstd, nmr, ve, bst, half_neg = (res[n] for n in ("ident", "mv", "rstd", "nmr", "ve", "bst", "half_neg"))
    WT, b100, gbb = res["WT"], res["b100"], res["gbb"]
    with ExitStack() as ctx:
        sb = lambda name, shape, dt=F32: ctx.enter_context(nc.sbuf_tensor(name, shape, dt))
        pb = lambda name: ctx.enter_context(nc.psum_tensor(name, [P, 512], F32))
        X = sb("X1", [P, NX, C])
        Hs = sb("Hs", [P, NX, C])
        raw = sb("raw", [P, 2, QT, ROW])
        rden = sb("rden", [P, 2, QT * H])
        th = sb("th", [P, U, CH * C])
        h1 = sb("h1", [P, U, CH * C])
        h2 = sb("h2", [P, U, CH * C])
        h2T = sb("h2T", [P, U, CH * C])
        cst = sb("cst", [P, U, CH, 6])
        cmv = sb("cmv", [P, U, CH, 2])
        cve = sb("cve", [P, U, CH])
        r100 = sb("r100", [P, U, CH])
        ps_x = [pb(f"ps_x{i}") for i in range(3)]
        ps_g = [pb(f"ps_g{i}") for i in range(U)]
        XB = [0, 1, 2, 0, 1]
        XD = [2, 2, 5, 3, 3]
        s_raw = [sem(f"s_raw{i}") for i in range(2)]
        s_norm = sem("s_norm")
        s_x1var = sem("s_x1var")
        s_x1root = sem("s_x1root")
        s_aff = sem("s_aff")
        s_tanh = sem("s_tanh")
        s_add = sem("s_add")
        s_silu = sem("s_silu")
        s_ve = sem("s_ve")
        s_r = sem("s_r")
        s_xp = sem("s_xp")
        s_h2T = sem("s_h2T")
        s_prod = sem("s_prod")
        s_dffn = sem("s_dffn")
        s_x1in = [sem(f"s_x1in{b}") for b in range(NT // QT)]
        s_biased = sem("s_biased")
        s_x1pad = sem("s_x1pad")
        s_bn = sem("s_bn")
        s_pffn = sem("s_pffn")
        s_fin = sem("s_fin")
        s_out = sem("s_out")
        TURNS = NC // U
        ALL = ITERS * NC

        def chunk_rows(ap, j):
            return ap[:, bass.ds(j * CH, CH), :].rearrange("p a c -> p (a c)")

        def iterate(eng, turn):
            turn(0, 0)
            turn(U, U)
            with eng.Fori(2, TURNS) as b:
                turn(b * U, b * U)
            with eng.Fori(1, ITERS) as it:
                with eng.Fori(0, TURNS) as b:
                    turn(it * NC + b * U, b * U)

        with nc.Block() as block:
            @block.sync
            def _(sp):
                for b in range(NT // QT):
                    if b >= 2:
                        sp.wait_ge(s_norm, b - 1)
                    sp.dma_start(raw[:, b % 2, :, :], agg[b * QT * P:(b + 1) * QT * P, :]
                                 .rearrange("(t p) c -> p t c", p=P)).then_inc(s_raw[b % 2], 16)
                for b in range(NT // QT):
                    full = min((b + 1) * QT, NT - 1)
                    sp.wait_ge(s_fin, b + 1)
                    sp.dma_start(out[b * QT * P:full * P, :].rearrange("(t p) c -> p t c", p=P), X[:, b * QT:full, :]).then_inc(s_out, 16)
                sp.dma_start(out[(NT - 1) * P:N, :], X[0:TAIL, NT - 1, :]).then_inc(s_out, 16)
                sp.wait_ge(s_out, 16 * (NT // QT + 1))

            @block.gpsimd
            def _(pool):
                ch = Chain(pool, s_pffn)
                nc.gpsimd.memset(X[:, NT - 1:NX, :], 0.0).then_inc(s_x1pad, 1)

                def biased(b):
                    hs = Hs[:, b * QT:(b + 1) * QT, :]
                    pool.wait_ge(s_norm, b + 1)
                    nc.gpsimd.tensor_tensor(hs, hs, gbb[:, :].unsqueeze(1).to_broadcast([P, QT, C]), ALU.add).then_inc(s_biased, 1)

                def roots(b):
                    t0, t1 = part_tiles(b)
                    pool.wait_ge(s_x1var, b + 1)
                    ch.add(nc.gpsimd.tensor_tensor(rstd[:, t0:t1], ve[:, t0:t1], half_neg[:, t0:t1], ALU.pow))
                    ch.wait()
                    ch.add(nc.gpsimd.tensor_scalar(rstd[:, t0:t1], rstd[:, t0:t1], HS, None, ALU.mult))
                    ch.wait()
                    ch.add(nc.gpsimd.tensor_tensor(nmr[:, t0:t1], rstd[:, t0:t1], mv[:, t0:t1, 0], ALU.mult))
                    ch.wait()
                    nc.gpsimd.tensor_scalar(nmr[:, t0:t1], nmr[:, t0:t1], -1.0, None, ALU.mult).then_inc(s_x1root, 1)

                for b in range(NT // QT):
                    biased(b)
                    if b >= 2:
                        roots(b - 2)
                roots(NT // QT - 2)
                roots(NT // QT - 1)

                def turn(q0, j0):
                    for u in range(U):
                        q = q0 + u
                        pool.wait_ge(s_tanh, q + 1)
                        wait_count(pool, s_silu, q + 1 - U)
                        pool.nop(nofuse=True)
                        nc.gpsimd.tensor_tensor(h1[:, u, :], chunk_rows(Hs, j0 + u), th[:, u, :], ALU.add).then_inc(s_add, 1)
                        if not (isinstance(q, int) and q < 3):
                            root(q - 3, (u - 3) % U)

                def root(q, u):
                    pool.wait_ge(s_ve, q + 1)
                    pool.wait_ge(s_aff, q + (NC + 1 - U))
                    nc.gpsimd.tensor_tensor(r100[:, u, :], cve[:, u, :], half_neg[:, 0:CH], ALU.pow).then_inc(s_r, 1)

                iterate(pool, turn)
                for q in range(ALL - 3, ALL):
                    root(q, q % U)

            @block.scalar
            def _(act):
                def silu(q, u):
                    act.wait_ge(s_add, q + 1)
                    wait_count(act, s_xp, q + 1 - U)
                    wait_count(act, s_ve, q + 1 - U)
                    nc.scalar.activation(h2[:, u, :], h1[:, u, :], ACT.Silu, scale=1.0 / HS).then_inc(s_silu, 1)

                def copy_t(q, u):
                    act.wait_ge(s_xp, q + 1)
                    wait_count(act, s_prod, q + 1 - U)
                    nc.scalar.activation(h2T[:, u, :], ps_x[XB[u]][:, :], ACT.Copy).then_inc(s_h2T, 1)

                def turn(q0, j0):
                    for u in range(U):
                        q = q0 + u
                        act.wait_ge(s_aff, q + 1)
                        wait_count(act, s_add, q + 1 - U)
                        act.nop(nofuse=True)
                        nc.scalar.activation(th[:, u, :], chunk_rows(Hs, j0 + u), ACT.Tanh, scale=1.0 / HS).then_inc(s_tanh, 1)
                        if not (isinstance(q, int) and q < 1):
                            silu(q - 1, (u - 1) % U)
                        if not (isinstance(q, int) and q < 3):
                            copy_t(q - 3, (u - 3) % U)

                act.wait_ge(s_x1pad, 1)
                for b in range(NT // QT):
                    load_part(act, x, X, b, s_x1in[b])
                for b in range(NT // QT):
                    t0, t1 = part_tiles(b)
                    act.wait_ge(s_x1root, b + 1)
                    for t in range(t0, t1):
                        last = nc.scalar.activation(Hs[:, t, :], X[:, t, :], ACT.Identity,
                                                    scale=rstd[:, t:t + 1], bias=nmr[:, t:t + 1])
                        if t % CH:
                            last.then_inc(s_aff, 1)
                iterate(act, turn)
                silu(ALL - 1, (ALL - 1) % U)
                for q in range(ALL - 3, ALL):
                    copy_t(q, q % U)

            @block.vector
            def _(dve):
                ch = Chain(dve, s_dffn)
                v = nc.vector
                v.memset(Hs[:, NT:NX, :], 0.0)
                ch.add(v.memset(cve[:, :, :], 0.0))
                ch.wait()

                def normed(b):
                    rw = raw[:, b % 2, :, :].rearrange("p t (h f) -> p (t h) f", h=H)
                    dve.wait_ge(s_raw[b % 2], (b // 2 + 1) * 16)
                    ch.add(v.reciprocal(rden[:, b % 2, :], rw[:, :, HID]))
                    ch.wait()
                    v.tensor_tensor(Hs[:, b * QT:(b + 1) * QT, :].rearrange("p t (h f) -> p (t h) f", h=H), rw[:, :, 0:HID],
                                    rden[:, b % 2, :].unsqueeze(2).to_broadcast([P, QT * H, HID]),
                                    ALU.mult).then_inc(s_norm, 1)

                def added(b):
                    t0, t1 = part_tiles(b)
                    hs = Hs[:, b * QT:(b + 1) * QT, :].rearrange("p t c -> p (t c)")
                    xs = X[:, b * QT:(b + 1) * QT, :].rearrange("p t c -> p (t c)")
                    dve.wait_ge(s_x1in[b], 16 if b < NT // QT - 1 else 32)
                    dve.wait_ge(s_biased, b + 1)
                    ch.add(v.scalar_tensor_tensor(out=xs, in0=hs, scalar=0.0, in1=xs, op0=ALU.max, op1=ALU.add))
                    ch.wait()
                    for t in range(t0, t1):
                        last = v.bn_stats(bst[:, t, :], X[:, t, :])
                    ch.add(last)
                    ch.wait()
                    for t in range(t0, t1):
                        last = v.bn_aggr(mv[:, t, :], bst[:, t, :])
                    ch.add(last)
                    ch.wait()
                    v.tensor_scalar(ve[:, t0:t1], mv[:, t0:t1, 1], EPS, None, ALU.add).then_inc(s_x1var, 1)

                for b in range(NT // QT):
                    normed(b)
                    if b:
                        added(b - 1)
                added(NT // QT - 1)

                def stats(q, u):
                    dve.wait_ge(s_silu, q + 1)
                    for a in range(CH):
                        last = v.bn_stats(cst[:, u, a, :], h2[:, u, a * C:(a + 1) * C])
                    last.then_inc(s_bn, 1)

                def moments(q, u):
                    dve.wait_ge(s_bn, 2 * q + 1)
                    dve.nop(nofuse=True)
                    for a in range(CH):
                        last = v.bn_aggr(cmv[:, u, a, :], cst[:, u, a, :])
                    last.then_inc(s_bn, 1)

                def variance(q, u):
                    dve.wait_ge(s_bn, 2 * q + 2)
                    wait_count(dve, s_r, q + 1 - U)
                    v.tensor_scalar(cve[:, u, :], cmv[:, u, :, 1], EPS, 1.0 / (HS * HS), ALU.add, ALU.mult).then_inc(s_ve, 1)

                def affine(q, j, u, a):
                    if a == 0:
                        dve.wait_ge(s_prod, q + 1)
                        dve.wait_ge(s_r, q + 1)
                    ins = v.scalar_tensor_tensor(out=Hs[:, bass.ds(j * CH + a, 1), :].rearrange("p a c -> p (a c)"),
                                                 in0=ps_g[u][:, a * C:(a + 1) * C],
                                                 scalar=r100[:, u, a:a + 1], in1=b100[:, :], op0=ALU.mult, op1=ALU.add)
                    if a == CH - 1:
                        ins.then_inc(s_aff, 1)

                LEAD = 3
                for q in range(LEAD):
                    stats(q, q)
                    moments(q, q)
                    variance(q, q)

                def turn(q0, j0, lead=U):
                    for u in range(U):
                        ahead = (q0 + (u + LEAD), (u + LEAD) % U)
                        if u < lead:
                            stats(*ahead)
                        affine(q0 + u, j0 + u, u, 0)
                        if u < lead:
                            moments(*ahead)
                        affine(q0 + u, j0 + u, u, 1)
                        if u < lead:
                            variance(*ahead)

                turn(0, 0)
                with dve.Fori(1, TURNS) as b:
                    turn(b * U, b * U)
                with dve.Fori(1, ITERS - 1) as it:
                    with dve.Fori(0, TURNS) as b:
                        turn(it * NC + b * U, b * U)
                with dve.Fori(0, TURNS - 1) as b:
                    turn(b * U + (ITERS - 1) * NC, b * U)
                turn(ALL - U, NC - U, lead=U - LEAD)
                dve.wait_ge(s_aff, NC + ALL)
                for b in range(NT // QT):
                    xs = X[:, b * QT:(b + 1) * QT, :].rearrange("p t c -> p (t c)")
                    hs = Hs[:, b * QT:(b + 1) * QT, :].rearrange("p t c -> p (t c)")
                    v.scalar_tensor_tensor(out=xs, in0=hs, scalar=1.0 / HS, in1=xs, op0=ALU.mult, op1=ALU.add).then_inc(s_fin, 1)

            @block.tensor
            def _(pe):
                def transposes(q, u):
                    pe.wait_ge(s_silu, q + 1)
                    wait_count(pe, s_h2T, q + 1 - XD[u])
                    for n in range(CH * 2):
                        last = nc.tensor.transpose(ps_x[XB[u]][:, n * P:(n + 1) * P], h2[:, u, n * P:(n + 1) * P], ident[:, :])
                    last.then_inc(s_xp, 1)

                def product(q, u):
                    pe.wait_ge(s_h2T, q + 1)
                    pe.wait_ge(s_aff, q + (NC + 1 - U))
                    for a in range(CH):
                        for k in range(2):
                            last = nc.tensor.matmul(ps_g[u][:, a * C:(a + 1) * C], h2T[:, u, (a * 2 + k) * P:(a * 2 + k + 1) * P],
                                                    WT[:, k, :], start=(k == 0), stop=(k == 1))
                    last.then_inc(s_prod, 1)

                def turn(q0, j0):
                    for u in range(U):
                        q = q0 + u
                        transposes(q, u)
                        if not (isinstance(q, int) and q < 2):
                            product(q - 2, (u - 2) % U)

                iterate(pe, turn)
                for q in range(ALL - 2, ALL):
                    product(q, q % U)


def kernel(x, src, dst, L0_gnn_W, L0_gnn_att_src, L0_gnn_att_dst, L0_gnn_bias,
           L0_ffn_ln_w, L0_ffn_ln_b, L0_ffn_W, L0_ffn_b):
    import numpy as np
    import concourse.bacc as bacc
    from concourse.bass_utils import run_bass_kernel_spmd

    arrays = {
        "x": x, "src": src, "dst": dst, "gnn_W": L0_gnn_W, "att_src": L0_gnn_att_src,
        "att_dst": L0_gnn_att_dst, "gnn_bias": L0_gnn_bias, "ln_w": L0_ffn_ln_w, "ln_b": L0_ffn_ln_b,
        "ffn_W": L0_ffn_W, "ffn_b": L0_ffn_b,
    }
    arrays = {n: np.ascontiguousarray(a) for n, a in arrays.items()}
    arrays["src"] = arrays["src"].view(np.uint32)
    nc = bacc.Bacc("TRN2", target_bir_lowering=False, num_devices=1)
    args = [nc.dram_tensor(n, a.shape, mybir.dt.from_np(a.dtype), kind="ExternalInput").ap() for n, a in arrays.items()]
    out = nc.dram_tensor("out", (N, C), F32, kind="ExternalOutput").ap()
    build(nc, *args, out)
    return run_bass_kernel_spmd(nc, [arrays], core_ids=[0]).results[0]["out"]
```
